# Optimizing a Trainium2 kernel written in Bass

```python
import numpy as np
import jax
import jax.numpy as jnp

def _softmax(x, axis=-1):
    return jax.nn.softmax(x, axis=axis)

def _gelu(x):
    return jax.nn.gelu(x, approximate=True)

def _silu(x):
    return jax.nn.silu(x)

def _sigmoid(x):
    return jax.nn.sigmoid(x)

def _layernorm(x, axis=-1, eps=1e-05):
    m = jnp.mean(x, axis=axis, keepdims=True)
    v = jnp.var(x, axis=axis, keepdims=True)
    return (x - m) / jnp.sqrt(v + eps)

def _scatter_add(tgt, idx, src, axis=0):
    return tgt.at[idx].add(src)

def _segment_sum(src, seg, n):
    return jax.ops.segment_sum(src, seg, n)
kernel_name = 'mk_recurrent_d1_jaxref_r4_0cc78c'

def setup_inputs(seed: int=0):
    np.random.seed(seed)
    _w = jnp.asarray

    def _L0_attn_setup():
        import jax, jax.numpy as jnp
        import numpy as np
        B, S, D = (2, 512, 1024)
        NH, NKV = (32, 8)
        HD = D // NH
        NREP = NH // NKV
        SCALE = HD ** (-0.5)
        key = jax.random.key(seed)
        kx, kq, kk, kv, ko = jax.random.split(key, 5)
        s = 0.02
        return {'x': jax.random.normal(kx, (B, S, D), dtype=jnp.float32), 'wq': jax.random.normal(kq, (D, NH * HD), dtype=jnp.float32) * s, 'wk': jax.random.normal(kk, (D, NKV * HD), dtype=jnp.float32) * s, 'wv': jax.random.normal(kv, (D, NKV * HD), dtype=jnp.float32) * s, 'wo': jax.random.normal(ko, (NH * HD, D), dtype=jnp.float32) * s}
    _L0_attn_in = _L0_attn_setup()

    def _L0_ffn_setup():
        import jax, jax.numpy as jnp
        import numpy as np
        B, S, D, O, E, R = (2, 1024, 1024, 1024, 8, 16)
        TOP_K = 2
        SCALING = 32.0 / 16.0
        key = jax.random.key(seed)
        k = jax.random.split(key, 6)
        x = jax.random.normal(k[0], (B, S, D), dtype=jnp.float32)
        W_base = jax.random.normal(k[1], (O, D), dtype=jnp.float32) * 0.02
        b_base = jax.random.normal(k[2], (O,), dtype=jnp.float32) * 0.02
        W_router = jax.random.normal(k[3], (E, D), dtype=jnp.float32) * 0.01
        lora_A = jax.random.normal(k[4], (E, R, D), dtype=jnp.float32) * (1.0 / np.sqrt(D))
        lora_B = jax.random.normal(k[5], (E, O, R), dtype=jnp.float32) * 0.02
        return {'x': x, 'W_base': W_base, 'b_base': b_base, 'W_router': W_router, 'lora_A': lora_A, 'lora_B': lora_B}
    _L0_ffn_in = _L0_ffn_setup()
    _d = {'L0_attn_x': _L0_attn_in['x'], 'L0_attn_wq': _L0_attn_in['wq'], 'L0_attn_wk': _L0_attn_in['wk'], 'L0_attn_wv': _L0_attn_in['wv'], 'L0_attn_wo': _L0_attn_in['wo'], 'L0_ffn_W_base': _L0_ffn_in['W_base'], 'L0_ffn_b_base': _L0_ffn_in['b_base'], 'L0_ffn_W_router': _L0_ffn_in['W_router'], 'L0_ffn_lora_A': _L0_ffn_in['lora_A'], 'L0_ffn_lora_B': _L0_ffn_in['lora_B']}
    _x0 = _d['L0_attn_x']
    _d['L0_attn_x'] = jax.random.normal(jax.random.fold_in(jax.random.key(seed), 1), (2, 2048, 1024), dtype=_x0.dtype)
    del _x0
    return _d

def reference(L0_attn_x, L0_attn_wq, L0_attn_wk, L0_attn_wv, L0_attn_wo, L0_ffn_W_base, L0_ffn_b_base, L0_ffn_W_router, L0_ffn_lora_A, L0_ffn_lora_B):

    def _L0_attn_ref(x, wq, wk, wv, wo):
        import jax, jax.numpy as jnp
        import numpy as np
        B, S, D = (2, 512, 1024)
        NH, NKV = (32, 8)
        HD = D // NH
        NREP = NH // NKV
        SCALE = HD ** (-0.5)
        b, s, _ = x.shape
        q = (x @ wq).reshape(b, s, NH, HD)
        k = (x @ wk).reshape(b, s, NKV, HD)
        v = (x @ wv).reshape(b, s, NKV, HD)
        k = jnp.repeat(k, NREP, axis=2)
        v = jnp.repeat(v, NREP, axis=2)
        scores = jnp.einsum('bihd,bjhd->bhij', q, k) * SCALE
        causal = jnp.tril(jnp.ones((s, s), dtype=bool))
        scores = jnp.where(causal, scores, jnp.finfo(scores.dtype).min)
        attn = jax.nn.softmax(scores, axis=-1)
        out = jnp.einsum('bhij,bjhd->bihd', attn, v)
        out = out.reshape(b, s, NH * HD)
        return out @ wo

    def _L0_ffn_ref(x, W_base, b_base, W_router, lora_A, lora_B):
        import jax, jax.numpy as jnp
        import numpy as np
        B, S, D, O, E, R = (2, 1024, 1024, 1024, 8, 16)
        TOP_K = 2
        SCALING = 32.0 / 16.0
        d = x.shape[-1]
        n_experts = W_router.shape[0]
        xf = x.reshape(-1, d)
        logits = xf @ W_router.T
        probs = jax.nn.softmax(logits, axis=-1)
        topk_p, topk_i = jax.lax.top_k(probs, TOP_K)
        topk_p = topk_p / jnp.sum(topk_p, axis=-1, keepdims=True)
        w = jnp.sum(jax.nn.one_hot(topk_i, n_experts, dtype=xf.dtype) * topk_p[..., None], axis=1)
        h = jnp.einsum('td,erd->ter', xf, lora_A)
        lora_out = jnp.einsum('ter,eor,te->to', h, lora_B, w) * SCALING
        base = x @ W_base.T + b_base
        return base + lora_out.reshape(x.shape[:-1] + (W_base.shape[0],))
    x = L0_attn_x
    xn = _layernorm(x, axis=-1)
    s = _L0_attn_ref(xn, L0_attn_wq, L0_attn_wk, L0_attn_wv, L0_attn_wo)
    g = _silu(_L0_ffn_ref(xn, L0_ffn_W_base, L0_ffn_b_base, L0_ffn_W_router, L0_ffn_lora_A, L0_ffn_lora_B))
    x = x + s * g
    return x

_drawn_inputs = setup_inputs


def setup_inputs(seed=0):
    import zlib

    import numpy as np

    out = dict(_drawn_inputs(seed))
    spreads = {}
    factors = {'L0_attn_wq': 8.0,
     'L0_attn_wk': 8.0,
     'L0_attn_wv': 3.862,
     'L0_attn_wo': 3.914,
     'L0_ffn_W_base': 4.694,
     'L0_ffn_b_base': 25.433,
     'L0_ffn_W_router': 8.0,
     'L0_ffn_lora_A': 8.0,
     'L0_ffn_lora_B': 8.0}
    for name, (base, spread) in spreads.items():
        noise = np.random.default_rng([zlib.crc32(name.encode()), seed]).standard_normal(out[name].shape)
        drawn = base * np.exp(spread * noise) if base else spread * noise
        out[name] = jnp.asarray(drawn.astype(out[name].dtype))
    for name, factor in factors.items():
        out[name] = (out[name] * factor).astype(out[name].dtype)
    return out
```

```python
from contextlib import ExitStack

import concourse.bass as bass
from concourse import mybir

FP32 = mybir.dt.float32
FP32R = mybir.dt.float32r
BF16 = mybir.dt.bfloat16
ALU = mybir.AluOpType
ACT = mybir.ActivationFunctionType
AX = mybir.AxisListType

P = 128
B, S, D = 2, 2048, 1024
T = B * S
KT = D // P
NH, NKV, HD = 32, 8, 32
NREP = NH // NKV
SCALE = float(HD) ** -0.5
E, R = 8, 16
EPS = 1e-5
LORA_SCALING = 2.0
MASKED = -1.0e38

CH = 512
TPC = CH // P
NCH = T // CH
CPB = S // CH
NG = B * NKV
NT = T // P

C_V, C_R, C_Q, C_K, C_A = 0, NKV * HD, NKV * HD + E, NKV * HD + E + NH * HD, NKV * HD + E + NH * HD + NKV * HD
WCOLS = C_A + E * R
WHALF = WCOLS // 2


class Step:

    def __init__(self, pair, u):
        self.pair, self.u = pair, u

    def lin(self, per_step, offset=0):
        return self.pair * (2 * per_step) + (self.u * per_step + offset)


def wait_apart(engine, semaphore, value, passed):
    engine.wait_ge(semaphore, value)
    engine.sem_inc(passed, 1)


def bcast(ap, axis, count):
    ap = ap.unsqueeze(axis)
    shape = list(ap.shape)
    shape[axis] = count
    return ap.to_broadcast(shape)


def project(nc, x, wall, sc, ident):
    ctx = ExitStack()
    with ctx:
        def sb(name, shape, dt=FP32):
            return ctx.enter_context(nc.sbuf_tensor(name, shape, dt))

        def sem(name):
            return ctx.enter_context(nc.semaphore(name))

        w_hi = sb("w_hi", [P, KT, WCOLS], FP32R)
        w_lo = sb("w_lo", [P, KT, WCOLS], FP32R)
        w_raw = sb("w_raw", [P, 2, WHALF])
        xt_hi = [sb(f"xt_hi{i}", [P, KT, CH], FP32R) for i in range(2)]
        xt_lo = [sb(f"xt_lo{i}", [P, KT, CH], FP32R) for i in range(2)]
        x_sb = sb("x_sb", [P, TPC, D])
        v_sb = sb("v_sb", [P, NKV, TPC, HD])
        out_hi = [sb(f"out_hi{i}", [P, CH], FP32R) for i in range(2)]
        out_lo = [sb(f"out_lo{i}", [P, CH], FP32R) for i in range(2)]
        hw = sb("hw", [P, CH])
        stats = sb("stats", [P, TPC, 2, 6])
        mv = sb("mv", [P, TPC, 2])
        var = sb("var", [P, TPC])
        std = sb("std", [P, TPC])
        inv = sb("inv", [P, 4, TPC])
        logits = sb("logits", [P, TPC, E])
        rest = sb("rest", [P, TPC, E])
        rank = sb("rank", [P, TPC, E])
        eq = sb("eq", [P, TPC, E])
        first = sb("first", [P, TPC, E])
        second = sb("second", [P, TPC, E])
        top = sb("top", [P, 8, TPC])
        acc = [ctx.enter_context(nc.psum_tensor(f"acc{i}", [P, 512], FP32)) for i in range(4)]
        turned = [ctx.enter_context(nc.psum_tensor(f"turned{i}", [P, 512], FP32)) for i in range(4)]

        passed = sem("p_passed")
        x_loaded = [sem(f"p_x_loaded{i}") for i in range(TPC)]
        w_loaded = [sem(f"p_w_loaded{i}") for i in range(2)]
        w_hi_ready = sem("p_w_hi_ready")
        w_lo_ready = sem("p_w_lo_ready")
        rank_ready = sem("p_rank_ready")
        var_ready = sem("p_var_ready")
        std_ready = sem("p_std_ready")
        ln_link = sem("p_ln_link")
        xn_ready = sem("p_xn_ready")
        turn_full = sem("p_turn_full")
        turn_hi = sem("p_turn_hi")
        turn_free = sem("p_turn_free")
        acc_full = sem("p_acc_full")
        acc_hi = sem("p_acc_hi")
        acc_free = sem("p_acc_free")
        gap_ready = sem("p_gap_ready")
        ratio_ready = sem("p_ratio_ready")
        rt_link = sem("p_rt_link")
        route_ready = sem("p_route_ready")
        hw_lo_ready = sem("p_hw_lo_ready")
        out_stored = [sem(f"p_out_stored{i}") for i in range(2)]
        v_stored = sem("p_v_stored")
        xt_stored = [sem(f"p_xt_stored{i}") for i in range(2)]

        NA = 16
        NTR = 2 * TPC
        NQ = NH * HD // P
        NK = NKV * HD // P
        NO = NQ + NK + 1
        NLN, NRT = 7, 17

        block = ctx.enter_context(nc.Block())

        def over_chunks(engine, pair_of_chunks):
            with engine.Fori(0, 2) as pair:
                pair_of_chunks(pair, 0, False)
            pair_of_chunks(2, 1, False)
            pair_of_chunks(3, 1, True)

        @block.sync
        def _(sp):
            def load_x(t, m):
                row = m * CH + t * P
                sp.dma_start(x_sb[:, t, :], x[bass.ds(row, P), :] if not isinstance(row, int) else x[row:row + P, :]) \
                  .then_inc(x_loaded[t], 16)

            def store_xt(m, u):
                wait_apart(sp, turn_free, m.lin(NTR, NTR + 4), passed)
                for dst, src in ((sc["xt_hi"], xt_hi[u]), (sc["xt_lo"], xt_lo[u])):
                    for t in range(TPC):
                        sp.dma_start(dst[:, bass.ds(m.lin(TPC, t), 1), :, :].squeeze(1),
                                     src[:, :, t * P:(t + 1) * P].bitcast(FP32)).then_inc(xt_stored[u], 16)

            for s in xt_stored:
                sp.sem_inc(s, 16 * 2 * TPC)
            for s in out_stored:
                sp.sem_inc(s, 32)
            sp.sem_inc(v_stored, 16)
            for t in range(TPC):
                load_x(t, 0)
            for t in range(TPC):
                sp.wait_ge(turn_full, 2 * t + 2)
                load_x(t, 1)
            store_xt(Step(0, 0), 0)

            def pair_of_chunks(pair, b, last):
                for u in range(2):
                    n = Step(pair, u)
                    col = n.lin(CH, -b * S)
                    wait_apart(sp, acc_free, n.lin(NA, TPC + 4), passed)
                    sp.dma_start(sc["v"][b, :, :, bass.ds(n.lin(TPC * HD, -b * CPB * TPC * HD), TPC * HD)]
                                 .rearrange("g p c -> p g c"),
                                 v_sb[:, :, :, :].rearrange("p g t d -> p g (t d)")).then_inc(v_stored, 16)
                    for j in range(NQ + NK):
                        s = (NO * u + j) % 2
                        wait_apart(sp, acc_free, n.lin(NA, TPC + 4 + j + 1), passed)
                        for part, src in (("hi", out_hi[s]), ("lo", out_lo[s])):
                            if j < NQ:
                                dst = sc["q_" + part][b, j, :, bass.ds(col, CH)]
                            else:
                                k4 = P // HD
                                dst = sc["k_" + part][b, (j - NQ) * k4:(j - NQ + 1) * k4, :, bass.ds(col, CH)] \
                                    .rearrange("g d c -> (g d) c")
                            sp.dma_start(dst, src[:, :].bitcast(FP32)).then_inc(out_stored[s], 16)
                        if j < NQ and j % 2 and not last:
                            t = j // 2
                            wait_apart(sp, turn_full, n.lin(NTR, NTR + 2 * t + 2), passed)
                            load_x(t, n.lin(1, 2))
                    if not (last and u == 1):
                        store_xt(Step(pair, 1) if u == 0 else Step(pair + 1, 0), 1 - u)
                    s = (NO * u + NO - 1) % 2
                    wait_apart(sp, hw_lo_ready, n.lin(1, 1), passed)
                    for part, src in (("hi", out_hi[s]), ("lo", out_lo[s])):
                        sp.dma_start(sc["hw_" + part][:, bass.ds(n.lin(CH), CH)], src[:, :].bitcast(FP32)) \
                          .then_inc(out_stored[s], 16)
            over_chunks(sp, pair_of_chunks)
            for s in range(2):
                sp.wait_ge(out_stored[s], 32 + 32 * (NO * NCH // 2))
                sp.wait_ge(xt_stored[s], 16 * 2 * TPC * (NCH // 2 + 1))
            sp.wait_ge(v_stored, 16 * (NCH + 1))

        @block.gpsimd
        def _(pool):
            for e in range(E):
                last = nc.gpsimd.memset(rank[:, :, e:e + 1], float(E - e))
            last.then_inc(rank_ready, 1)

        @block.scalar
        def _(act):
            def turn_high(m, u, j):
                t, half = j // 2, j % 2
                act.wait_ge(turn_full, m.lin(NTR, j + 1))
                if j == 0:
                    act.wait_ge(xt_stored[u], m.pair * (16 * 2 * TPC) + 16 * 2 * TPC)
                nc.scalar.activation(xt_hi[u][:, half * 4:half * 4 + 4, t * P:(t + 1) * P],
                                     turned[j % 4][:, :].rearrange("p (k c) -> p k c", k=4), ACT.Copy) \
                    .then_inc(turn_hi, 1)

            def deviation(m):
                act.wait_ge(var_ready, m.lin(1, 1))
                nc.scalar.activation(std[:, :], var[:, :], ACT.Sqrt).then_inc(std_ready, 1)

            def load_w(i):
                k, half = i // 2, i % 2
                act.dma_start(w_raw[:, half, :], wall[k * P:(k + 1) * P, half * WHALF:(half + 1) * WHALF]) \
                   .then_inc(w_loaded[half], 16)

            load_w(0)
            load_w(1)
            zero = Step(0, 0)
            deviation(zero)
            for j in range(NTR):
                turn_high(zero, 0, j)
            for i in range(2 * KT):
                k, half = i // 2, i % 2
                act.wait_ge(w_loaded[half], 16 * (k + 1))
                nc.scalar.activation(w_hi[:, k, half * WHALF:(half + 1) * WHALF], w_raw[:, half, :], ACT.Copy) \
                    .then_inc(w_hi_ready, 1)
                if i >= 1 and i + 1 < 2 * KT:
                    act.wait_ge(w_lo_ready, i)
                    load_w(i + 1)

            def pair_of_chunks(pair, b, last):
                for u in range(2):
                    n = Step(pair, u)
                    m = Step(pair, 1) if u == 0 else Step(pair + 1, 0)
                    ahead = not (last and u == 1)
                    for t in range(TPC):
                        act.wait_ge(acc_full, n.lin(NA, t + 1))
                        if t == 0:
                            act.wait_ge(v_stored, n.lin(16, 16))
                        nc.scalar.activation(v_sb[:, :, t, :], acc[t % 4][:, C_V:C_R].rearrange("p (g d) -> p g d", g=NKV),
                                             ACT.Copy).then_inc(acc_hi, 1)
                        if t == 1 and ahead:
                            deviation(m)
                    for j in range(NQ + NK):
                        item, use = TPC + j, NO * u + j
                        act.wait_ge(acc_full, n.lin(NA, item + 1))
                        act.wait_ge(out_stored[use % 2], pair * (32 * NO) + (32 * (use // 2) + 32))
                        nc.scalar.activation(out_hi[use % 2][:, :], acc[item % 4][:, :], ACT.Copy,
                                             scale=SCALE if j < NQ else 1.0).then_inc(acc_hi, 1)
                        if j < NQ and ahead:
                            turn_high(m, 1 - u, j)
                        if j == 2:
                            act.wait_ge(gap_ready, n.lin(1, 1))
                            nc.scalar.activation(top[:, 3, :], top[:, 2, :], ACT.Exp).then_inc(ratio_ready, 1)
                    act.wait_ge(acc_full, n.lin(NA, NA))
                    nc.scalar.activation(hw[:, :], acc[(NA - 1) % 4][:, :], ACT.Copy).then_inc(acc_hi, 1)
                    use = NO * u + NO - 1
                    act.wait_ge(acc_free, n.lin(NA, NA + 4))
                    act.wait_ge(out_stored[use % 2], pair * (32 * NO) + (32 * (use // 2) + 32))
                    nc.scalar.activation(out_hi[use % 2][:, :], hw[:, :], ACT.Copy).then_inc(acc_hi, 1)
            over_chunks(act, pair_of_chunks)

        @block.vector
        def _(dve):
            def linker(sem_, start):
                done = [0]

                def link(ins):
                    done[0] += 1
                    ins.then_inc(sem_, 1)
                    dve.wait_ge(sem_, start(done[0]))
                return link, done

            def variances(m):
                link, done = linker(ln_link, lambda k: m.lin(NLN, k))
                for t in range(TPC):
                    dve.wait_ge(x_loaded[t], m.lin(16, 16))
                    for h in range(2):
                        ins = nc.vector.bn_stats(stats[:, t, h, :], x_sb[:, t, h * 512:(h + 1) * 512])
                link(ins)
                dve.sem_inc(passed, 1)
                for t in range(TPC):
                    ins = nc.vector.bn_aggr(mv[:, t, :], stats[:, t, :, :])
                link(ins)
                nc.vector.tensor_scalar(var[:, :], mv[:, :, 1], EPS, None, ALU.add).then_inc(var_ready, 1)

            def normalise(m):
                link, done = linker(ln_link, lambda k: m.lin(NLN, 2 + k))
                dve.wait_ge(std_ready, m.lin(1, 1))
                link(nc.vector.reciprocal(inv[:, 0, :], std[:, :]))
                link(nc.vector.tensor_mul(inv[:, 1, :], inv[:, 0, :], inv[:, 0, :]))
                link(nc.vector.tensor_mul(inv[:, 2, :], inv[:, 1, :], var[:, :]))
                link(nc.vector.tensor_scalar(inv[:, 1, :], inv[:, 2, :], -0.5, 1.5, ALU.mult, ALU.add))
                link(nc.vector.tensor_mul(inv[:, 3, :], inv[:, 0, :], inv[:, 1, :]))
                assert 2 + done[0] == NLN
                for t in range(TPC):
                    nc.vector.tensor_scalar(x_sb[:, t, :], x_sb[:, t, :], mv[:, t, 0:1], inv[:, 3, t:t + 1],
                                            ALU.subtract, ALU.mult).then_inc(xn_ready, 1)

            def turn_low(m, u, j):
                t, half = j // 2, j % 2
                dve.wait_ge(turn_hi, m.lin(NTR, j + 1))
                at = (slice(None), slice(half * 4, half * 4 + 4), slice(t * P, (t + 1) * P))
                nc.vector.tensor_sub(xt_lo[u][at], turned[j % 4][:, :].rearrange("p (k c) -> p k c", k=4),
                                     xt_hi[u][at].bitcast(FP32)).then_inc(turn_free, 1)

            dve.sem_inc(turn_free, 4)
            dve.sem_inc(acc_free, 4)
            zero = Step(0, 0)
            variances(zero)
            normalise(zero)
            for j in range(NTR):
                turn_low(zero, 0, j)
            for i in range(2 * KT):
                k, half = i // 2, i % 2
                dve.wait_ge(w_hi_ready, i + 1)
                cols = slice(half * WHALF, (half + 1) * WHALF)
                nc.vector.tensor_sub(w_lo[:, k, cols], w_raw[:, half, :], w_hi[:, k, cols].bitcast(FP32)) \
                    .then_inc(w_lo_ready, 1)
            dve.wait_ge(rank_ready, 1)

            def winner(link, values, best, mask):
                link(nc.vector.tensor_reduce(best, values[:, :, :], AX.X, ALU.max))
                link(nc.vector.tensor_tensor(eq[:, :, :], values[:, :, :], bcast(best, 2, E), ALU.is_equal))
                link(nc.vector.tensor_mul(eq[:, :, :], eq[:, :, :], rank[:, :, :]))
                link(nc.vector.tensor_reduce(top[:, 4, :], eq[:, :, :], AX.X, ALU.max))
                link(nc.vector.tensor_tensor(mask[:, :, :], eq[:, :, :], bcast(top[:, 4, :], 2, E), ALU.is_equal))

            def pair_of_chunks(pair, b, last):
                for u in range(2):
                    n = Step(pair, u)
                    m = Step(pair, 1) if u == 0 else Step(pair + 1, 0)
                    ahead = not (last and u == 1)
                    if ahead:
                        variances(m)
                    for t in range(TPC):
                        dve.wait_ge(acc_hi, n.lin(NA, t + 1))
                        nc.vector.tensor_copy(logits[:, t, :], acc[t % 4][:, C_R:C_Q]).then_inc(acc_free, 1)
                    if ahead:
                        normalise(m)
                    link, done = linker(rt_link, lambda k: n.lin(NRT, k))
                    dve.wait_ge(acc_free, n.lin(NA, TPC + 4))
                    winner(link, logits, top[:, 0, :], first)
                    link(nc.vector.scalar_tensor_tensor(rest[:, :, :], first[:, :, :], MASKED, logits[:, :, :],
                                                        ALU.mult, ALU.add))
                    winner(link, rest, top[:, 1, :], second)
                    nc.vector.tensor_sub(top[:, 2, :], top[:, 1, :], top[:, 0, :]).then_inc(gap_ready, 1)
                    for j in range(NQ + NK):
                        item, use = TPC + j, NO * u + j
                        dve.wait_ge(acc_hi, n.lin(NA, item + 1))
                        nc.vector.scalar_tensor_tensor(out_lo[use % 2][:, :], acc[item % 4][:, :],
                                                       SCALE if j < NQ else 1.0, out_hi[use % 2][:, :].bitcast(FP32),
                                                       ALU.mult, ALU.subtract).then_inc(acc_free, 1)
                        if j < NQ and ahead:
                            turn_low(m, 1 - u, j)
                        if j == 3:
                            dve.wait_ge(ratio_ready, n.lin(1, 1))
                            link(nc.vector.tensor_scalar(top[:, 5, :], top[:, 3, :], 1.0, None, ALU.add))
                            link(nc.vector.reciprocal(top[:, 6, :], top[:, 5, :]))
                            link(nc.vector.tensor_scalar(top[:, 6, :], top[:, 6, :], LORA_SCALING, None, ALU.mult))
                            link(nc.vector.tensor_mul(top[:, 7, :], top[:, 6, :], top[:, 3, :]))
                            link(nc.vector.tensor_mul(first[:, :, :], first[:, :, :], bcast(top[:, 6, :], 2, E)))
                            link(nc.vector.tensor_mul(second[:, :, :], second[:, :, :], bcast(top[:, 7, :], 2, E)))
                            nc.vector.tensor_add(hw[:, :].rearrange("p (t e r) -> p t e r", t=TPC, e=E),
                                                 bcast(first[:, :, :], 3, R), bcast(second[:, :, :], 3, R)) \
                                .then_inc(route_ready, 1)
                            assert done[0] == NRT, done
                    dve.wait_ge(acc_hi, n.lin(NA, NA - 1))
                    nc.vector.tensor_mul(hw[:, :], acc[(NA - 2) % 4][:, :], hw[:, :]).then_inc(acc_free, 2)
                    dve.wait_ge(acc_hi, n.lin(NA, NA))
                    use = NO * u + NO - 1
                    nc.vector.tensor_sub(out_lo[use % 2][:, :], hw[:, :], out_hi[use % 2][:, :].bitcast(FP32)) \
                        .then_inc(hw_lo_ready, 1)
            over_chunks(dve, pair_of_chunks)

        @block.tensor
        def _(pe):
            def turn(m, j):
                t, half = j // 2, j % 2
                pe.wait_ge(xn_ready, m.lin(TPC, t + 1))
                pe.wait_ge(turn_free, m.lin(NTR, j + 1))
                for i in range(4):
                    k = half * 4 + i
                    ins = nc.tensor.transpose(turned[j % 4][:, i * P:(i + 1) * P], x_sb[:, t, k * P:(k + 1) * P], ident[:, :])
                ins.then_inc(turn_full, 1)

            def product(out, lhs, rhs):
                for k in range(KT):
                    (lh, ll), (rh, rl) = lhs(k), rhs(k)
                    nc.tensor.matmul(out, lh, rh, start=(k == 0), stop=False)
                    nc.tensor.matmul(out, lh, rl, start=False, stop=False)
                    ins = nc.tensor.matmul(out, ll, rh, start=False, stop=(k == KT - 1))
                return ins

            zero = Step(0, 0)
            for j in range(NTR):
                turn(zero, j)
            pe.wait_ge(w_lo_ready, 2 * KT)

            def pair_of_chunks(pair, b, last):
                for u in range(2):
                    n = Step(pair, u)
                    m = Step(pair, 1) if u == 0 else Step(pair + 1, 0)
                    ahead = not (last and u == 1)

                    def weights(k, c0, c1):
                        return w_hi[:, k, c0:c1], w_lo[:, k, c0:c1]

                    def tokens(k, c0=0, c1=CH):
                        return xt_hi[u][:, k, c0:c1], xt_lo[u][:, k, c0:c1]

                    pe.wait_ge(turn_free, n.lin(NTR, NTR + 4))
                    for t in range(TPC):
                        pe.wait_ge(acc_free, n.lin(NA, t + 1))
                        product(acc[t % 4][:, C_V:C_Q], lambda k: tokens(k, t * P, (t + 1) * P),
                                lambda k: weights(k, C_V, C_Q)).then_inc(acc_full, 1)
                    for j in range(NQ + NK + 1):
                        item = TPC + j
                        c0 = C_Q + j * P
                        pe.wait_ge(acc_free, n.lin(NA, item + 1))
                        product(acc[item % 4][:, :], lambda k: weights(k, c0, c0 + P), tokens).then_inc(acc_full, 1)
                        if j < NQ and ahead:
                            turn(m, j)
                    pe.wait_ge(route_ready, n.lin(1, 1))
                    pe.wait_ge(acc_free, n.lin(NA, NA))
                    for t in range(TPC):
                        ins = nc.tensor.matmul(acc[(NA - 1) % 4][:, t * P:(t + 1) * P], hw[:, t * P:(t + 1) * P],
                                               ident[:, :], start=True, stop=True)
                    ins.then_inc(acc_full, 1)
            over_chunks(pe, pair_of_chunks)


def pieces_of(c):
    out = []
    for i in range(TPC):
        keys = (TPC * c + i + 1) * P
        for h in range(NREP):
            for p in range(-(-keys // 1024)):
                out.append((i, h, p, min(1024, keys - 1024 * p)))
    return out


def stage(c):
    steps = TPC * (c + 1)
    pieces = list(enumerate(pieces_of((c + 1) % CPB)))
    slots = 4 * max(steps - 3, 0)
    order, given = [], 0
    if not slots or c == 0:
        order += [("S", n, p) for n, p in pieces]
        given = len(pieces)
    for j in range(steps):
        for h in range(NREP):
            order.append(("T", j, h))
            due = len(pieces) if 4 * j + h + 1 >= slots else -(-len(pieces) * (4 * j + h + 1) // slots)
            while given < due:
                order.append(("S", *pieces[given]))
                given += 1
        if j:
            order.append(("V", j - 1))
        if j == max(steps - 3, 0):
            order.append(("M",))
        if j == steps - 1:
            order.append(("R",))
    order += [("V", steps - 1), ("O",)]
    return order


STAGES = [stage(c) for c in range(CPB)]
PIECES = [len(pieces_of((c + 1) % CPB)) for c in range(CPB)]
NP0 = len(pieces_of(0))
NPG = sum(PIECES)
SLOTS = [n + 2 for n in PIECES]
NSG = sum(SLOTS)
NTG = sum(NREP * TPC * (c + 1) for c in range(CPB))
NJG = NTG // NREP


def attend(nc, sc, ident, ident_b, mask_ij, mask_ji):
    ctx = ExitStack()
    with ctx:
        def sb(name, shape, dt=FP32):
            return ctx.enter_context(nc.sbuf_tensor(name, shape, dt))

        def sem(name):
            return ctx.enter_context(nc.semaphore(name))

        K1 = 3 * HD
        q_st = [sb(f"q_st{i}", [K1 + 1, NREP, CH], FP32R) for i in range(CPB)]
        k_st = [sb(f"k_st{i}", [K1 + 1, S], FP32R) for i in range(2)]
        v_st = [sb(f"v_st{i}", [P, S // P, HD]) for i in range(2)]
        probs = [sb(f"probs{i}", [P, NREP, CH]) for i in range(4)]
        neg_max = sb("neg_max", [P, 2, 16])
        low_max = sb("low_max", [P, 16])
        sums = sb("sums", [P, 2, 16])
        shift = sb("shift", [P, 16], FP32R)
        diff = sb("diff", [P, 2, 16])
        corr = sb("corr", [P, 2, 16])
        total = sb("total", [P, 16])
        inv_sum = sb("inv_sum", [P, 16])
        inv_wide = sb("inv_wide", [P, TPC, NREP * HD])
        row = [sb(f"row{i}", [16, P]) for i in range(2)]
        spread = [sb(f"spread{i}", [P, CH]) for i in range(2)]
        o_sb = [sb(f"o_sb{i}", [P, CH]) for i in range(2)]
        rows_ps = [ctx.enter_context(nc.psum_tensor(f"rows_ps{i}", [P, 1024], FP32)) for i in range(2)]
        cols_ps = [ctx.enter_context(nc.psum_tensor(f"cols_ps{i}", [P, CH], FP32)) for i in range(2)]
        o_ps = ctx.enter_context(nc.psum_tensor("o_ps", [P, CH], FP32))

        passed = sem("a_passed")
        q_loaded = [sem(f"a_q_loaded{i}") for i in range(CPB)]
        k_loaded = [sem(f"a_k_loaded{i}") for i in range(2)]
        v_loaded = [sem(f"a_v_loaded{i}") for i in range(2)]
        ones_ready = sem("a_ones_ready")
        rows_full = sem("a_rows_full")
        rows_free = sem("a_rows_free")
        max_ready = sem("a_max_ready")
        fin_link = sem("a_fin_link")
        shift_ready = sem("a_shift_ready")
        corr_ready = sem("a_corr_ready")
        inv_ready = sem("a_inv_ready")
        row_moved = [sem(f"a_row_moved{i}") for i in range(2)]
        cols_full = sem("a_cols_full")
        probs_ready = sem("a_probs_ready")
        values_done = sem("a_values_done")
        o_ready = sem("a_o_ready")
        o_stored = [sem(f"a_o_stored{i}") for i in range(2)]

        block = ctx.enter_context(nc.Block())
        P_OFF = [NP0 + sum(PIECES[:c]) for c in range(CPB)]
        S_OFF = [NP0 + 2 + sum(SLOTS[:c]) for c in range(CPB)]
        T_OFF = [NREP * TPC * c * (c + 1) // 2 for c in range(CPB)]
        J_OFF = [TPC * c * (c + 1) // 2 for c in range(CPB)]
        NPAIR = NG // 2
        N_LINK = sum(3 + 2 * (p > 16) for p in PIECES)
        N_LINK0 = 3

        def over_groups(engine, pair_of_groups):
            with engine.Fori(0, NPAIR - 1) as pair:
                pair_of_groups(pair, False)
            pair_of_groups(NPAIR - 1, True)

        @block.sync
        def _(sp):
            def load_q(n, c):
                for i, part in enumerate(("hi", "lo", "hi")):
                    src = sc["q_" + part].rearrange("b g (h d) c -> (b g) d h c", d=HD)
                    sp.dma_start(q_st[c][i * HD:(i + 1) * HD, :, :].bitcast(FP32),
                                 src[bass.ds(n, 1), :, :, c * CH:(c + 1) * CH].squeeze(0)).then_inc(q_loaded[c], 16)

            def load_kv(n, u):
                for i, part in enumerate(("hi", "hi", "lo")):
                    src = sc["k_" + part].rearrange("b g d c -> (b g) d c")
                    sp.dma_start(k_st[u][i * HD:(i + 1) * HD, :].bitcast(FP32), src[bass.ds(n, 1), :, :].squeeze(0)) \
                      .then_inc(k_loaded[u], 16)
                src = sc["v"].rearrange("b g p c -> (b g) p c")
                sp.dma_start(v_st[u][:, :, :].rearrange("p j d -> p (j d)"), src[bass.ds(n, 1), :, :].squeeze(0)) \
                  .then_inc(v_loaded[u], 16)

            def move_row(free, c):
                sp.wait_ge(rows_free, free)
                sp.dma_start(q_st[c][K1:K1 + 1, :, :].bitcast(FP32), row[c % 2][:, :]).then_inc(row_moved[c % 2], 16)

            for s in o_stored:
                sp.sem_inc(s, 16)
            load_kv(0, 0)
            load_q(0, 0)
            load_q(0, 1)
            move_row(2 + NP0 + 1, 0)

            def pair_of_groups(pair, last):
                for u in range(2):
                    n, ahead = Step(pair, u), not (last and u == 1)
                    for c in range(CPB):
                        done = {0: 0, 1: 0, 2: TPC, 3: 3 * TPC}[c]
                        if c < 2 or ahead:
                            wait_apart(sp, values_done, n.lin(NJG, done + 4), passed)
                            if c < 2:
                                load_q(n.lin(1), c + 2)
                            else:
                                load_q(n.lin(1, 1), c - 2)
                        if c == 0 and ahead:
                            load_kv(n.lin(1, 1), 1 - u)
                        if c < 3 or ahead:
                            move_row(n.lin(NSG, 2 + S_OFF[c] + PIECES[c] + 1), (c + 1) % CPB)
                        wait_apart(sp, o_ready, n.lin(CPB, c + 2), passed)
                        dst = sc["o"].rearrange("b g p c -> (b g) p c")
                        sp.dma_start(dst[bass.ds(n.lin(1), 1), :, c * CH:(c + 1) * CH].squeeze(0), o_sb[c % 2][:, :]) \
                          .then_inc(o_stored[c % 2], 16)
            over_groups(sp, pair_of_groups)
            for s in range(2):
                sp.wait_ge(o_stored[s], 16 + 16 * (CPB * NG // 2))

        @block.gpsimd
        def _(pool):
            for i in range(2):
                ins = nc.gpsimd.memset(k_st[i][K1:K1 + 1, :].bitcast(FP32), 1.0)
            ins.then_inc(ones_ready, 1)

        def stages_of(pair, last):
            for u in range(2):
                for c in range(CPB):
                    ahead = not (last and u == 1 and c == CPB - 1)
                    yield Step(pair, u), u, c, ahead

        def first_stage():
            return [("S", i, p) for i, p in enumerate(pieces_of(0))] + [("M",), ("R",)]

        @block.tensor
        def _(pe):
            def row_scores(value, n_slot, kbuf, c, i, h, p, keys, qcount, kcount):
                pe.wait_ge(rows_free, value + 1)
                out = rows_ps[n_slot % 2]
                for c0 in range(0, keys, CH):
                    c1 = min(keys, c0 + CH)
                    diagonal = 1024 * p + c1 == (TPC * c + i + 1) * P
                    ins = nc.tensor.matmul(out[:, c0:c1], q_st[c][0:K1, h, i * P:(i + 1) * P],
                                           k_st[kbuf][0:K1, 1024 * p + c0:1024 * p + c1], start=True, stop=not diagonal)
                    if diagonal:
                        ins = nc.tensor.matmul(out[:, c1 - P:c1], ident_b[:, :], mask_ij[:, :], start=False, stop=True)
                ins.then_inc(rows_full, 1)

            def turn_shift(value, n_slot, chunk_count):
                pe.wait_ge(shift_ready, chunk_count)
                pe.wait_ge(rows_free, value + 1)
                nc.tensor.transpose(rows_ps[n_slot % 2][0:16, 0:P], shift[:, :].bitcast(FP32), ident[:, :]) \
                    .then_inc(rows_full, 1)

            def spread_inverse(value, n_slot, chunk_count):
                pe.wait_ge(inv_ready, chunk_count)
                pe.wait_ge(rows_free, value + 1)
                for i in range(TPC):
                    ins = nc.tensor.matmul(rows_ps[n_slot % 2][:, i * P:(i + 1) * P], inv_wide[:, i, :],
                                           ident[:, :], start=True, stop=True)
                ins.then_inc(rows_full, 1)

            pe.sem_inc(values_done, 4)
            pe.wait_ge(ones_ready, 1)
            pe.wait_ge(q_loaded[0], 48)
            pe.wait_ge(k_loaded[0], 48)
            for s, op in enumerate(first_stage()):
                if op[0] == "S":
                    row_scores(s, s, 0, 0, *op[2], None, None)
                elif op[0] == "M":
                    turn_shift(s, s, 1)
                else:
                    spread_inverse(s, s, 1)

            def pair_of_groups(pair, last):
                for n, u, c, ahead in stages_of(pair, last):
                    cn = (c + 1) % CPB
                    kbuf = u if c < 3 else 1 - u
                    slot = 0
                    for op in STAGES[c]:
                        kind = op[0]
                        if kind in "SMR" and not ahead:
                            continue
                        if kind in "SMR":
                            value = n.lin(NSG, S_OFF[c] + slot)
                        if kind == "S":
                            if slot == 0:
                                pe.wait_ge(q_loaded[cn], n.lin(48, 48 if c < 3 else 96))
                                if c == 3:
                                    pe.wait_ge(k_loaded[1 - u], pair * 48 + (48 if u == 0 else 96))
                            row_scores(value, slot, kbuf, cn, *op[2], None, None)
                        elif kind == "M":
                            turn_shift(value, slot, n.lin(CPB, c + 2))
                        elif kind == "R":
                            spread_inverse(value, slot, n.lin(CPB, c + 2))
                        elif kind == "T":
                            j, h = op[1:]
                            q0 = max(0, j - TPC * c) * P
                            if j == 0 and h == 0:
                                pe.wait_ge(row_moved[c % 2], n.lin(32, 16 * (c // 2 + 1)))
                            index = T_OFF[c] + NREP * j + h
                            pe.wait_ge(probs_ready, n.lin(NTG, index + 1))
                            out = cols_ps[h % 2]
                            diagonal = j >= TPC * c
                            ins = nc.tensor.matmul(out[:, q0:CH], k_st[u][:, j * P:(j + 1) * P], q_st[c][:, h, q0:CH],
                                                   start=True, stop=not diagonal)
                            if diagonal:
                                ins = nc.tensor.matmul(out[:, q0:q0 + P], ident_b[:, :], mask_ji[:, :],
                                                       start=False, stop=True)
                            ins.then_inc(cols_full, 1)
                        elif kind == "V":
                            j = op[1]
                            q0 = max(0, j - TPC * c) * P
                            if j == 0:
                                pe.wait_ge(o_ready, n.lin(CPB, c + 1))
                                if c == 0:
                                    pe.wait_ge(v_loaded[u], pair * 16 + 16)
                            pe.wait_ge(probs_ready, n.lin(NTG, T_OFF[c] + NREP * (j + 1) + 2))
                            for h in range(NREP):
                                ins = nc.tensor.matmul(o_ps[h * HD:(h + 1) * HD, q0:CH], v_st[u][:, j, :],
                                                       probs[j % 4][:, h, q0:CH], start=(j == 0),
                                                       stop=(j == TPC * (c + 1) - 1), tile_position=(0, h * HD))
                            ins.then_inc(values_done, 1)
                        if kind in "SMR":
                            slot += 1
            over_groups(pe, pair_of_groups)

        @block.scalar
        def _(act):
            def piece_sum(value, n_slot, piece_count, i, h, p, keys):
                act.wait_ge(max_ready, piece_count)
                r = h * TPC + i
                at = rows_ps[n_slot % 2][:, 0:keys]
                nc.scalar.activation(at, at, ACT.Exp, bias=neg_max[:, p, r:r + 1], accum_out=sums[:, p, r:r + 1]) \
                    .then_inc(rows_free, 1)

            def shift_row(n_slot, chunk_count, np_, par, full):
                act.wait_ge(shift_ready, chunk_count)
                nc.scalar.activation(corr[:, 0:np_, :], diff[:, 0:np_, :], ACT.Exp).then_inc(corr_ready, 1)
                act.wait_ge(rows_full, full)
                nc.scalar.activation(row[par][:, :], rows_ps[n_slot % 2][0:16, 0:P], ACT.Copy) \
                    .then_inc(rows_free, 1)

            def spread_out(n_slot, par, full, o_count):
                act.wait_ge(rows_full, full)
                act.wait_ge(o_ready, o_count)
                nc.scalar.activation(spread[par][:, :], rows_ps[n_slot % 2][:, 0:CH], ACT.Copy).then_inc(rows_free, 1)

            act.sem_inc(rows_free, 2)
            act.sem_inc(probs_ready, 2)
            for s, op in enumerate(first_stage()):
                if op[0] == "S":
                    piece_sum(s, s, s + 1, *op[2])
                elif op[0] == "M":
                    shift_row(s, 1, 1, 0, s + 1)
                else:
                    spread_out(s, 0, s + 1, 1)

            def pair_of_groups(pair, last):
                for n, u, c, ahead in stages_of(pair, last):
                    cn = (c + 1) % CPB
                    np_ = PIECES[c] // 16
                    slot = 0
                    for op in STAGES[c]:
                        kind = op[0]
                        if kind in "SMR":
                            if not ahead:
                                continue
                            full = n.lin(NSG, S_OFF[c] + slot + 1)
                        if kind == "S":
                            piece_sum(None, slot, n.lin(NPG, P_OFF[c] + op[1] + 1), *op[2])
                        elif kind == "M":
                            shift_row(slot, n.lin(CPB, c + 2), np_, cn % 2, full)
                        elif kind == "R":
                            spread_out(slot, cn % 2, full, n.lin(CPB, c + 1))
                        elif kind == "T":
                            j, h = op[1:]
                            q0 = max(0, j - TPC * c) * P
                            act.wait_ge(cols_full, n.lin(NTG, T_OFF[c] + NREP * j + h + 1))
                            if h == 0:
                                act.wait_ge(values_done, n.lin(NJG, J_OFF[c] + j + 1))
                            nc.scalar.activation(probs[j % 4][:, h, q0:CH], cols_ps[h % 2][:, q0:CH], ACT.Exp) \
                                .then_inc(probs_ready, 1)
                        if kind in "SMR":
                            slot += 1
            over_groups(act, pair_of_groups)

        @block.vector
        def _(dve):
            links = [0]

            def piece_max(n_slot, full, i, h, p, keys):
                dve.wait_ge(rows_full, full)
                r = h * TPC + i
                nc.vector.tensor_reduce(neg_max[:, p, r:r + 1], rows_ps[n_slot % 2][:, 0:keys], AX.X, ALU.max,
                                        negate=True).then_inc(max_ready, 1)

            def linked(ins, value):
                links[0] += 1
                ins.then_inc(fin_link, 1)
                dve.wait_ge(fin_link, value(links[0]))

            def shifts(np_, max_count, value):
                dve.wait_ge(max_ready, max_count)
                low = neg_max[:, 0, :]
                if np_ == 2:
                    linked(nc.vector.tensor_tensor(low_max[:, :], neg_max[:, 0, :], neg_max[:, 1, :], ALU.min), value)
                    low = low_max[:, :]
                linked(nc.vector.tensor_copy(shift[:, :], low), value)
                nc.vector.tensor_sub(diff[:, 0:np_, :], bcast(shift[:, :].bitcast(FP32), 1, np_), neg_max[:, 0:np_, :]) \
                    .then_inc(shift_ready, 1)

            def inverse_sums(np_, chunk_count, value):
                dve.wait_ge(corr_ready, chunk_count)
                linked(nc.vector.tensor_mul(corr[:, 0:np_, :], corr[:, 0:np_, :], sums[:, 0:np_, :]), value)
                of = corr[:, 0, :]
                if np_ == 2:
                    linked(nc.vector.tensor_add(total[:, :], corr[:, 0, :], corr[:, 1, :]), value)
                    of = total[:, :]
                linked(nc.vector.reciprocal(inv_sum[:, :], of), value)
                for i in range(TPC):
                    ins = nc.vector.tensor_copy(inv_wide[:, i, :].rearrange("p (h d) -> p h d", h=NREP),
                                                bcast(inv_sum[:, :].rearrange("p (h i) -> p h i", h=NREP)[:, :, i], 2, HD))
                ins.then_inc(inv_ready, 1)

            dve.sem_inc(o_ready, 1)
            for s, op in enumerate(first_stage()):
                if op[0] == "S":
                    piece_max(s, s + 1, *op[2])
                elif op[0] == "M":
                    shifts(1, NP0, lambda k: k)
                else:
                    inverse_sums(1, 1, lambda k: k)
            assert links[0] == N_LINK0

            def pair_of_groups(pair, last):
                for n, u, c, ahead in stages_of(pair, last):
                    cn = (c + 1) % CPB
                    np_ = PIECES[c] // 16
                    if c == 0:
                        links[0] = 0
                    value = lambda k: n.lin(N_LINK, N_LINK0 + k)
                    slot = 0
                    for op in STAGES[c]:
                        kind = op[0]
                        if kind in "SMR" and not ahead:
                            continue
                        if kind == "S":
                            piece_max(slot, n.lin(NSG, S_OFF[c] + slot + 1), *op[2])
                        elif kind == "M":
                            shifts(np_, n.lin(NPG, P_OFF[c] + PIECES[c]), value)
                        elif kind == "R":
                            inverse_sums(np_, n.lin(CPB, c + 2), value)
                        elif kind == "O":
                            dve.wait_ge(values_done, n.lin(NJG, J_OFF[c] + TPC * (c + 1) + 4))
                            if c == 0:
                                dve.wait_ge(rows_free, n.lin(NSG, S_OFF[0] + 2))
                            else:
                                dve.wait_ge(rows_free, n.lin(NSG, S_OFF[c] + 2))
                            dve.wait_ge(o_stored[c % 2], n.lin(32, 16 * (c // 2) + 16))
                            nc.vector.tensor_mul(o_sb[c % 2][:, :], o_ps[:, :], spread[c % 2][:, :]).then_inc(o_ready, 1)
                        if kind in "SMR":
                            slot += 1
                    if ahead and c == CPB - 1:
                        assert links[0] == N_LINK, links
            over_groups(dve, pair_of_groups)


def split_weights(nc, block_act, block_dve, raw, hi, lo):
    pass


def gate(nc, wb, b_base, lb, sc):
    ctx = ExitStack()
    with ctx:
        def sb(name, shape, dt=FP32):
            return ctx.enter_context(nc.sbuf_tensor(name, shape, dt))

        def sem(name):
            return ctx.enter_context(nc.semaphore(name))

        NW = KT + 1
        HALF = D // 2
        w_hi = sb("g_w_hi", [P, NW, D], FP32R)
        w_lo = sb("g_w_lo", [P, NW, D], FP32R)
        w_raw = sb("g_w_raw", [P, 2, D])
        bias = sb("g_bias", [P, D])
        t_hi = [sb(f"g_t_hi{i}", [P, NW, P], FP32R) for i in range(2)]
        t_lo = [sb(f"g_t_lo{i}", [P, NW, P], FP32R) for i in range(2)]
        z = sb("g_z", [P, 2, HALF])
        th = sb("g_th", [P, 2, HALF])
        g = sb("g_g", [P, 2, HALF])
        acc = [ctx.enter_context(nc.psum_tensor(f"g_acc{i}", [P, HALF], FP32)) for i in range(2)]
        passed = sem("g_passed")
        w_loaded = [sem(f"g_w_loaded{i}") for i in range(2)]
        bias_loaded = sem("g_bias_loaded")
        w_hi_ready = sem("g_w_hi_ready")
        w_lo_ready = sem("g_w_lo_ready")
        t_loaded = [sem(f"g_t_loaded{i}") for i in range(2)]
        acc_full = sem("g_acc_full")
        z_ready = sem("g_z_ready")
        th_ready = sem("g_th_ready")
        g_ready = sem("g_g_ready")
        g_stored = [sem(f"g_g_stored{i}") for i in range(2)]
        block = ctx.enter_context(nc.Block())
        NPAIR = NT // 2

        @block.sync
        def _(sp):
            for s in g_stored:
                sp.sem_inc(s, 16)
            sp.dma_start(bias[:, :], b_base.partition_broadcast(P)).then_inc(bias_loaded, 16)

            def load(i, u):
                for part, dst in (("hi", t_hi[u]), ("lo", t_lo[u])):
                    sp.dma_start(dst[:, 0:KT, :].bitcast(FP32), sc["xt_" + part][:, bass.ds(i, 1), :, :].squeeze(1)) \
                      .then_inc(t_loaded[u], 16)
                    sp.dma_start(dst[:, KT, :].bitcast(FP32), sc["hw_" + part][:, bass.ds(i * P, P)]) \
                      .then_inc(t_loaded[u], 16)

            def pair_of_tiles(pair, last):
                for u in range(2):
                    n = Step(pair, u)
                    for half in range(2):
                        wait_apart(sp, g_ready, n.lin(2, half + 1), passed)
                        sp.dma_start(sc["g"][bass.ds(n.lin(P), P), half * HALF:(half + 1) * HALF], g[:, half, :]) \
                          .then_inc(g_stored[half], 16)
                    if not last:
                        load(n.lin(1, 2), u)
            load(0, 0)
            load(1, 1)
            with sp.Fori(0, NPAIR - 1) as pair:
                pair_of_tiles(pair, False)
            pair_of_tiles(NPAIR - 1, True)
            for s in g_stored:
                sp.wait_ge(s, 16 * (NT + 1))

        @block.scalar
        def _(act):
            def load_w(k):
                act.dma_start(w_raw[:, k % 2, :], wb[k * P:(k + 1) * P, :] if k < KT else lb[:, :]) \
                   .then_inc(w_loaded[k % 2], 16)
            load_w(0)
            load_w(1)
            for k in range(NW):
                act.wait_ge(w_loaded[k % 2], 16 * (k // 2 + 1))
                nc.scalar.activation(w_hi[:, k, :], w_raw[:, k % 2, :], ACT.Copy).then_inc(w_hi_ready, 1)
                if 1 <= k < NW - 1:
                    act.wait_ge(w_lo_ready, k)
                    load_w(k + 1)
            with act.Fori(0, NPAIR) as pair:
                for u in range(2):
                    n = Step(pair, u)
                    for half in range(2):
                        act.wait_ge(z_ready, n.lin(2, half + 3))
                        nc.scalar.activation(th[:, half, :], z[:, half, :], ACT.Tanh, scale=0.5).then_inc(th_ready, 1)

        @block.vector
        def _(dve):
            dve.sem_inc(z_ready, 2)
            for k in range(NW):
                dve.wait_ge(w_hi_ready, k + 1)
                nc.vector.tensor_sub(w_lo[:, k, :], w_raw[:, k % 2, :], w_hi[:, k, :].bitcast(FP32)).then_inc(w_lo_ready, 1)
            dve.wait_ge(bias_loaded, 16)
            with dve.Fori(0, NPAIR) as pair:
                for u in range(2):
                    n = Step(pair, u)
                    for half in range(2):
                        dve.wait_ge(acc_full, n.lin(2, half + 1))
                        nc.vector.tensor_add(z[:, half, :], acc[half][:, :], bias[:, half * HALF:(half + 1) * HALF]) \
                            .then_inc(z_ready, 1)
                        dve.wait_ge(th_ready, n.lin(2, half + 1))
                        dve.wait_ge(g_stored[half], n.lin(16, 16))
                        nc.vector.scalar_tensor_tensor(g[:, half, :], th[:, half, :], 1.0, z[:, half, :], ALU.add, ALU.mult) \
                            .then_inc(g_ready, 1)

        @block.tensor
        def _(pe):
            pe.wait_ge(w_lo_ready, NW)
            with pe.Fori(0, NPAIR) as pair:
                for u in range(2):
                    n = Step(pair, u)
                    pe.wait_ge(t_loaded[u], pair * 64 + 64)
                    for half in range(2):
                        pe.wait_ge(z_ready, n.lin(2, half + 1))
                        cols = slice(half * HALF, (half + 1) * HALF)
                        for k in range(NW):
                            nc.tensor.matmul(acc[half][:, :], t_hi[u][:, k, :], w_hi[:, k, cols], start=(k == 0), stop=False)
                            nc.tensor.matmul(acc[half][:, :], t_hi[u][:, k, :], w_lo[:, k, cols], start=False, stop=False)
                            ins = nc.tensor.matmul(acc[half][:, :], t_lo[u][:, k, :], w_hi[:, k, cols], start=False,
                                                   stop=(k == NW - 1))
                        ins.then_inc(acc_full, 1)


def output(nc, x, wo, sc, out):
    ctx = ExitStack()
    with ctx:
        def sb(name, shape, dt=FP32):
            return ctx.enter_context(nc.sbuf_tensor(name, shape, dt))

        def sem(name):
            return ctx.enter_context(nc.semaphore(name))

        HALF = D // 2
        w_hi = sb("o_w_hi", [P, KT, D], FP32R)
        w_lo = sb("o_w_lo", [P, KT, D], FP32R)
        w_raw = sb("o_w_raw", [P, 2, D])
        o_raw = [sb(f"o_raw{i}", [P, KT, P]) for i in range(2)]
        t_hi = [sb(f"o_t_hi{i}", [P, KT, P], FP32R) for i in range(2)]
        t_lo = [sb(f"o_t_lo{i}", [P, KT, P], FP32R) for i in range(2)]
        x_sb = sb("o_x", [P, 2, D])
        g_sb = sb("o_g", [P, 2, D])
        prod = sb("o_prod", [P, 2, HALF])
        y = sb("o_y", [P, 2, HALF])
        acc = [ctx.enter_context(nc.psum_tensor(f"o_acc{i}", [P, HALF], FP32)) for i in range(2)]
        passed = sem("o_passed")
        w_loaded = [sem(f"o_w_loaded{i}") for i in range(2)]
        w_hi_ready = sem("o_w_hi_ready")
        w_lo_ready = sem("o_w_lo_ready")
        t_loaded = [sem(f"o_t_loaded{i}") for i in range(2)]
        xg_loaded = [sem(f"o_xg_loaded{i}") for i in range(2)]
        t_hi_ready = sem("o_t_hi_ready")
        t_lo_ready = sem("o_t_lo_ready")
        acc_full = sem("o_acc_full")
        prod_ready = sem("o_prod_ready")
        y_ready = sem("o_y_ready")
        y_stored = [sem(f"o_y_stored{i}") for i in range(2)]
        block = ctx.enter_context(nc.Block())
        NPAIR = NT // 2
        o_src = sc["o"].rearrange("b g p c -> p b g c")

        @block.sync
        def _(sp):
            for s in y_stored:
                sp.sem_inc(s, 16)

            def load(i, b, u):
                sp.dma_start(o_raw[u][:, :, :], o_src[:, b, :, bass.ds(i * P - b * S, P)]).then_inc(t_loaded[u], 16)
                sp.dma_start(x_sb[:, u, :], x[bass.ds(i * P, P), :]).then_inc(xg_loaded[u], 16)
                sp.dma_start(g_sb[:, u, :], sc["g"][bass.ds(i * P, P), :]).then_inc(xg_loaded[u], 16)

            def pair_of_tiles(pair, b, last):
                for u in range(2):
                    n = Step(pair, u)
                    for half in range(2):
                        wait_apart(sp, y_ready, n.lin(2, half + 1), passed)
                        sp.dma_start(out[bass.ds(n.lin(P), P), half * HALF:(half + 1) * HALF], y[:, half, :]) \
                          .then_inc(y_stored[half], 16)
                    if not last:
                        load(n.lin(1, 2), b, u)
            load(0, 0, 0)
            load(1, 0, 1)
            with sp.Fori(0, NPAIR // 2 - 1) as pair:
                pair_of_tiles(pair, 0, False)
            with sp.Fori(NPAIR // 2 - 1, NPAIR - 1) as pair:
                pair_of_tiles(pair, 1, False)
            pair_of_tiles(NPAIR - 1, 1, True)
            for s in y_stored:
                sp.wait_ge(s, 16 * (NT + 1))

        @block.scalar
        def _(act):
            def load_w(k):
                act.dma_start(w_raw[:, k % 2, :], wo[k * P:(k + 1) * P, :]).then_inc(w_loaded[k % 2], 16)

            def high(n, u):
                act.wait_ge(t_loaded[u], n.pair * 16 + 16)
                nc.scalar.activation(t_hi[u][:, :, :], o_raw[u][:, :, :], ACT.Copy).then_inc(t_hi_ready, 1)
            load_w(0)
            load_w(1)
            for k in range(KT):
                act.wait_ge(w_loaded[k % 2], 16 * (k // 2 + 1))
                nc.scalar.activation(w_hi[:, k, :], w_raw[:, k % 2, :], ACT.Copy).then_inc(w_hi_ready, 1)
                if 1 <= k < KT - 1:
                    act.wait_ge(w_lo_ready, k)
                    load_w(k + 1)
            high(Step(0, 0), 0)
            high(Step(0, 1), 1)
            with act.Fori(0, NPAIR - 1) as pair:
                for u in range(2):
                    act.wait_ge(acc_full, Step(pair, u).lin(2, 2))
                    high(Step(pair + 1, u), u)

        @block.vector
        def _(dve):
            def low(n, u):
                dve.wait_ge(t_hi_ready, n.lin(1, 1))
                nc.vector.tensor_sub(t_lo[u][:, :, :], o_raw[u][:, :, :], t_hi[u][:, :, :].bitcast(FP32)) \
                    .then_inc(t_lo_ready, 1)

            def finish(n, u):
                for half in range(2):
                    cols = slice(half * HALF, (half + 1) * HALF)
                    dve.wait_ge(acc_full, n.lin(2, half + 1))
                    if half == 0:
                        dve.wait_ge(xg_loaded[u], n.pair * 32 + 32)
                    nc.vector.scalar_tensor_tensor(prod[:, half, :], acc[half][:, :], 0.5, g_sb[:, u, cols],
                                                   ALU.mult, ALU.mult).then_inc(prod_ready, 1)
                    dve.wait_ge(prod_ready, n.lin(2, half + 3))
                    dve.wait_ge(y_stored[half], n.lin(16, 16))
                    nc.vector.tensor_add(y[:, half, :], prod[:, half, :], x_sb[:, u, cols]).then_inc(y_ready, 1)
            dve.sem_inc(prod_ready, 2)
            for k in range(KT):
                dve.wait_ge(w_hi_ready, k + 1)
                nc.vector.tensor_sub(w_lo[:, k, :], w_raw[:, k % 2, :], w_hi[:, k, :].bitcast(FP32)).then_inc(w_lo_ready, 1)
            low(Step(0, 0), 0)
            low(Step(0, 1), 1)
            with dve.Fori(0, NPAIR - 1) as pair:
                for u in range(2):
                    finish(Step(pair, u), u)
                    low(Step(pair + 1, u), u)
            for u in range(2):
                finish(Step(NPAIR - 1, u), u)

        @block.tensor
        def _(pe):
            pe.wait_ge(w_lo_ready, KT)
            with pe.Fori(0, NPAIR) as pair:
                for u in range(2):
                    n = Step(pair, u)
                    pe.wait_ge(t_lo_ready, n.lin(1, 1))
                    for half in range(2):
                        pe.wait_ge(prod_ready, n.lin(2, half + 1))
                        cols = slice(half * HALF, (half + 1) * HALF)
                        for k in range(KT):
                            nc.tensor.matmul(acc[half][:, :], t_hi[u][:, k, :], w_hi[:, k, cols], start=(k == 0), stop=False)
                            nc.tensor.matmul(acc[half][:, :], t_hi[u][:, k, :], w_lo[:, k, cols], start=False, stop=False)
                            ins = nc.tensor.matmul(acc[half][:, :], t_lo[u][:, k, :], w_hi[:, k, cols], start=False,
                                                   stop=(k == KT - 1))
                        ins.then_inc(acc_full, 1)


def program(nc, x, wall, wo, wb, b_base, lb, out):
    def scratch(name, *shape):
        return nc.dram_tensor("scratch_" + name, shape, FP32, kind="Internal").ap()

    sc = {}
    for part in ("hi", "lo"):
        sc["xt_" + part] = scratch("xt_" + part, P, NT, KT, P)
        sc["q_" + part] = scratch("q_" + part, B, NKV, P, S)
        sc["k_" + part] = scratch("k_" + part, B, NKV, HD, S)
        sc["hw_" + part] = scratch("hw_" + part, P, T)
    sc["v"] = scratch("v", B, NKV, P, S // P * HD)
    sc["o"] = scratch("o", B, NKV, P, S)
    sc["g"] = scratch("g", T, D)

    with ExitStack() as ctx:
        ident = ctx.enter_context(nc.sbuf_tensor("ident", [P, P], FP32))
        ident_b = ctx.enter_context(nc.sbuf_tensor("ident_b", [P, P], BF16))
        mask_ij = ctx.enter_context(nc.sbuf_tensor("mask_ij", [P, P], BF16))
        mask_ji = ctx.enter_context(nc.sbuf_tensor("mask_ji", [P, P], BF16))
        made = ctx.enter_context(nc.semaphore("made"))
        with nc.Block() as block:
            @block.gpsimd
            def _(pool):
                for m in (ident, ident_b, mask_ij, mask_ji):
                    nc.gpsimd.memset(m[:, :], 0.0).then_inc(made, 1)
                pool.wait_ge(made, 4)
                for m in (ident, ident_b):
                    nc.gpsimd.affine_select(out=m[:, :], in_=m[:, :], compare_op=ALU.not_equal, fill=1.0, base=0,
                                            pattern=[[-1, P]], channel_multiplier=1).then_inc(made, 1)
                nc.gpsimd.affine_select(out=mask_ij[:, :], in_=mask_ij[:, :], compare_op=ALU.is_ge, fill=MASKED, base=0,
                                        pattern=[[-1, P]], channel_multiplier=1).then_inc(made, 1)
                nc.gpsimd.affine_select(out=mask_ji[:, :], in_=mask_ji[:, :], compare_op=ALU.is_ge, fill=MASKED, base=0,
                                        pattern=[[1, P]], channel_multiplier=-1).then_inc(made, 1)
                pool.wait_ge(made, 8)
        project(nc, x, wall, sc, ident)
        attend(nc, sc, ident, ident_b, mask_ij, mask_ji)
        gate(nc, wb, b_base, lb, sc)
        output(nc, x, wo, sc, out)


def kernel(L0_attn_x, L0_attn_wq, L0_attn_wk, L0_attn_wv, L0_attn_wo, L0_ffn_W_base, L0_ffn_b_base, L0_ffn_W_router,
           L0_ffn_lora_A, L0_ffn_lora_B):
    import numpy as np
    import concourse.bacc as bacc
    from concourse.bass_utils import run_bass_kernel_spmd

    arrays = {
        "x": np.ascontiguousarray(L0_attn_x).reshape(T, D),
        "wall": np.concatenate([np.asarray(L0_attn_wv), np.asarray(L0_ffn_W_router).T, np.asarray(L0_attn_wq),
                                np.asarray(L0_attn_wk), np.asarray(L0_ffn_lora_A).reshape(E * R, D).T], axis=1),
        "wo": np.ascontiguousarray(L0_attn_wo),
        "wb": np.ascontiguousarray(np.asarray(L0_ffn_W_base).T),
        "b_base": np.ascontiguousarray(L0_ffn_b_base),
        "lb": np.ascontiguousarray(np.asarray(L0_ffn_lora_B).transpose(0, 2, 1)).reshape(E * R, D),
    }
    nc = bacc.Bacc("TRN2", target_bir_lowering=False, num_devices=1)
    args = [nc.dram_tensor("in_" + k, a.shape, FP32, kind="ExternalInput").ap() for k, a in arrays.items()]
    out = nc.dram_tensor("out", (T, D), FP32, kind="ExternalOutput").ap()
    program(nc, *args, out)
    res = run_bass_kernel_spmd(nc, [{"in_" + k: a for k, a in arrays.items()}], core_ids=[0])
    return res.results[0]["out"].reshape(B, S, D)
```

```python
from contextlib import ExitStack

import concourse.bass as bass
from concourse import mybir

FP32 = mybir.dt.float32
FP32R = mybir.dt.float32r
BF16 = mybir.dt.bfloat16
ALU = mybir.AluOpType
ACT = mybir.ActivationFunctionType
AX = mybir.AxisListType

P = 128
B, S, D = 2, 2048, 1024
T = B * S
KT = D // P
NH, NKV, HD = 32, 8, 32
NREP = NH // NKV
SCALE = float(HD) ** -0.5
E, R = 8, 16
EPS = 1e-5
LORA_SCALING = 2.0
MASKED = -1.0e38

CH = 512
TPC = CH // P
NCH = T // CH
CPB = S // CH
NG = B * NKV
NT = T // P

C_V, C_R, C_Q, C_K, C_A = 0, NKV * HD, NKV * HD + E, NKV * HD + E + NH * HD, NKV * HD + E + NH * HD + NKV * HD
WCOLS = C_A + E * R
C_SPLIT = C_Q + 4 * P


class Step:

    def __init__(self, pair, u):
        self.pair, self.u = pair, u

    def lin(self, per_step, offset=0):
        return self.pair * (2 * per_step) + (self.u * per_step + offset)


def wait_apart(engine, semaphore, value, passed):
    engine.wait_ge(semaphore, value)
    engine.sem_inc(passed, 1)


def bcast(ap, axis, count):
    ap = ap.unsqueeze(axis)
    shape = list(ap.shape)
    shape[axis] = count
    return ap.to_broadcast(shape)


def project(nc, x, wall, sc, ident):
    ctx = ExitStack()
    with ctx:
        def sb(name, shape, dt=FP32):
            return ctx.enter_context(nc.sbuf_tensor(name, shape, dt))

        def sem(name):
            return ctx.enter_context(nc.semaphore(name))

        w_hi = sb("w_hi", [P, KT, WCOLS], FP32R)
        w_lo = sb("w_lo", [P, KT, WCOLS], FP32R)
        WPART = max(C_SPLIT, WCOLS - C_SPLIT)
        with nc.sbuf_tensor("w_raw", [P, 8, WPART], FP32) as w_raw:
            pass
        xt = {(part, i): sb(f"xt_{part}{i}", [P, KT, CH], FP32R) for i in (1, 0) for part in ("hi", "lo")}
        xt_hi, xt_lo = ([xt[part, i] for i in range(2)] for part in ("hi", "lo"))
        x_sb = sb("x_sb", [P, TPC, D])
        v_sb = sb("v_sb", [P, NKV, TPC, HD])
        out_hi = [sb(f"out_hi{i}", [P, CH], FP32R) for i in range(2)]
        out_lo = [sb(f"out_lo{i}", [P, CH], FP32R) for i in range(2)]
        hw = sb("hw", [P, CH])
        stats = sb("stats", [P, TPC, 2, 6])
        mv = sb("mv", [P, TPC, 2])
        var = sb("var", [P, TPC])
        std = sb("std", [P, TPC])
        inv = sb("inv", [P, 4, TPC])
        logits = sb("logits", [P, TPC, E])
        rest = sb("rest", [P, TPC, E])
        rank = sb("rank", [P, TPC, E])
        eq = sb("eq", [P, TPC, E])
        first = sb("first", [P, TPC, E])
        second = sb("second", [P, TPC, E])
        top = sb("top", [P, 8, TPC])
        acc = [ctx.enter_context(nc.psum_tensor(f"acc{i}", [P, 512], FP32)) for i in range(4)]
        turned = [ctx.enter_context(nc.psum_tensor(f"turned{i}", [P, 512], FP32)) for i in range(4)]

        passed = sem("p_passed")
        x_loaded = [sem(f"p_x_loaded{i}") for i in range(TPC)]
        w_loaded = [sem(f"p_w_loaded{i}") for i in range(8)]
        w_hi_ready = sem("p_w_hi_ready")
        w_lo_ready = sem("p_w_lo_ready")
        rank_ready = sem("p_rank_ready")
        var_ready = sem("p_var_ready")
        std_ready = sem("p_std_ready")
        ln_link = sem("p_ln_link")
        xn_ready = sem("p_xn_ready")
        turn_full = sem("p_turn_full")
        turn_hi = sem("p_turn_hi")
        turn_free = sem("p_turn_free")
        acc_full = sem("p_acc_full")
        acc_hi = sem("p_acc_hi")
        acc_free = sem("p_acc_free")
        gap_ready = sem("p_gap_ready")
        ratio_ready = sem("p_ratio_ready")
        rt_link = sem("p_rt_link")
        route_ready = sem("p_route_ready")
        hw_lo_ready = sem("p_hw_lo_ready")
        out_stored = [sem(f"p_out_stored{i}") for i in range(2)]
        v_stored = sem("p_v_stored")
        xt_stored = [sem(f"p_xt_stored{i}") for i in range(2)]

        NA = 16
        NTR = 2 * TPC
        NQ = NH * HD // P
        NK = NKV * HD // P
        NO = NQ + NK + 1
        NLN, NRT = 7, 17

        def w_piece(i):
            half, k = i // KT, i % KT
            c0, c1 = ((0, C_SPLIT), (C_SPLIT, WCOLS))[half]
            slot = i % 8
            return k, slice(c0, c1), slot, w_raw[:, slot, 0:c1 - c0]

        def load_w(engine, i):
            k, cols, slot, raw = w_piece(i)
            engine.dma_start(raw, wall[k * P:(k + 1) * P, cols]).then_inc(w_loaded[slot], 16)

        block = ctx.enter_context(nc.Block())

        def over_chunks(engine, pair_of_chunks):
            with engine.Fori(0, 2) as pair:
                pair_of_chunks(pair, 0, False)
            pair_of_chunks(2, 1, False)
            pair_of_chunks(3, 1, True)

        @block.sync
        def _(sp):
            def load_x(t, m):
                row = m * CH + t * P
                sp.dma_start(x_sb[:, t, :], x[bass.ds(row, P), :] if not isinstance(row, int) else x[row:row + P, :]) \
                  .then_inc(x_loaded[t], 16)

            def store_xt(m, u):
                wait_apart(sp, turn_free, m.lin(NTR, NTR + 4), passed)
                for dst, src in ((sc["xt_hi"], xt_hi[u]), (sc["xt_lo"], xt_lo[u])):
                    for t in range(TPC):
                        sp.dma_start(dst[:, bass.ds(m.lin(TPC, t), 1), :, :].squeeze(1),
                                     src[:, :, t * P:(t + 1) * P].bitcast(FP32)).then_inc(xt_stored[u], 16)

            for s in xt_stored:
                sp.sem_inc(s, 16 * 2 * TPC)
            for s in out_stored:
                sp.sem_inc(s, 32)
            sp.sem_inc(v_stored, 16)
            for t in range(TPC):
                load_x(t, 0)
            for i in range(8):
                load_w(sp, i)
            for t in range(TPC):
                sp.wait_ge(turn_full, 2 * t + 2)
                load_x(t, 1)
            store_xt(Step(0, 0), 0)

            def pair_of_chunks(pair, b, last):
                for u in range(2):
                    n = Step(pair, u)
                    col = n.lin(CH, -b * S)
                    wait_apart(sp, acc_free, n.lin(NA, TPC + 4), passed)
                    sp.dma_start(sc["v"][b, :, :, bass.ds(n.lin(TPC * HD, -b * CPB * TPC * HD), TPC * HD)]
                                 .rearrange("g p c -> p g c"),
                                 v_sb[:, :, :, :].rearrange("p g t d -> p g (t d)")).then_inc(v_stored, 16)
                    for j in range(NQ + NK):
                        s = (NO * u + j) % 2
                        wait_apart(sp, acc_free, n.lin(NA, TPC + 4 + j + 1), passed)
                        for part, src in (("hi", out_hi[s]), ("lo", out_lo[s])):
                            if j < NQ:
                                dst = sc["q_" + part][b, j, :, bass.ds(col, CH)]
                            else:
                                k4 = P // HD
                                dst = sc["k_" + part][b, (j - NQ) * k4:(j - NQ + 1) * k4, :, bass.ds(col, CH)] \
                                    .rearrange("g d c -> (g d) c")
                            sp.dma_start(dst, src[:, :].bitcast(FP32)).then_inc(out_stored[s], 16)
                        if j < NQ and j % 2 and not last:
                            t = j // 2
                            wait_apart(sp, turn_full, n.lin(NTR, NTR + 2 * t + 2), passed)
                            load_x(t, n.lin(1, 2))
                    if not (last and u == 1):
                        store_xt(Step(pair, 1) if u == 0 else Step(pair + 1, 0), 1 - u)
                    s = (NO * u + NO - 1) % 2
                    wait_apart(sp, hw_lo_ready, n.lin(1, 1), passed)
                    for part, src in (("hi", out_hi[s]), ("lo", out_lo[s])):
                        sp.dma_start(sc["hw_" + part][:, bass.ds(n.lin(CH), CH)], src[:, :].bitcast(FP32)) \
                          .then_inc(out_stored[s], 16)
            over_chunks(sp, pair_of_chunks)
            for s in range(2):
                sp.wait_ge(out_stored[s], 32 + 32 * (NO * NCH // 2))
                sp.wait_ge(xt_stored[s], 16 * 2 * TPC * (NCH // 2 + 1))
            sp.wait_ge(v_stored, 16 * (NCH + 1))

        @block.gpsimd
        def _(pool):
            for e in range(E):
                last = nc.gpsimd.memset(rank[:, :, e:e + 1], float(E - e))
            last.then_inc(rank_ready, 1)

        @block.scalar
        def _(act):
            def turn_high(m, u, j):
                t, half = j // 2, j % 2
                act.wait_ge(turn_full, m.lin(NTR, j + 1))
                if j == 0:
                    act.wait_ge(xt_stored[u], m.pair * (16 * 2 * TPC) + 16 * 2 * TPC)
                nc.scalar.activation(xt_hi[u][:, half * 4:half * 4 + 4, t * P:(t + 1) * P],
                                     turned[j % 4][:, :].rearrange("p (k c) -> p k c", k=4), ACT.Copy) \
                    .then_inc(turn_hi, 1)

            def deviation(m):
                act.wait_ge(var_ready, m.lin(1, 1))
                nc.scalar.activation(std[:, :], var[:, :], ACT.Sqrt).then_inc(std_ready, 1)

            zero = Step(0, 0)
            deviation(zero)
            for j in range(NTR):
                turn_high(zero, 0, j)
            for i in range(2 * KT):
                k, cols, slot, raw = w_piece(i)
                act.wait_ge(w_loaded[slot], 16 * (i // 8 + 1))
                nc.scalar.activation(w_hi[:, k, cols], raw, ACT.Copy).then_inc(w_hi_ready, 1)
                if i >= 1 and i + 7 < 2 * KT:
                    act.wait_ge(w_lo_ready, i)
                    load_w(act, i + 7)
            act.wait_ge(w_lo_ready, 2 * KT)

            def pair_of_chunks(pair, b, last):
                for u in range(2):
                    n = Step(pair, u)
                    m = Step(pair, 1) if u == 0 else Step(pair + 1, 0)
                    ahead = not (last and u == 1)
                    for t in range(TPC):
                        act.wait_ge(acc_full, n.lin(NA, t + 1))
                        if t == 0:
                            act.wait_ge(v_stored, n.lin(16, 16))
                        nc.scalar.activation(v_sb[:, :, t, :], acc[t % 4][:, C_V:C_R].rearrange("p (g d) -> p g d", g=NKV),
                                             ACT.Copy).then_inc(acc_hi, 1)
                        if t == 1 and ahead:
                            deviation(m)
                    for j in range(NQ + NK):
                        item, use = TPC + j, NO * u + j
                        act.wait_ge(acc_full, n.lin(NA, item + 1))
                        act.wait_ge(out_stored[use % 2], pair * (32 * NO) + (32 * (use // 2) + 32))
                        nc.scalar.activation(out_hi[use % 2][:, :], acc[item % 4][:, :], ACT.Copy,
                                             scale=SCALE if j < NQ else 1.0).then_inc(acc_hi, 1)
                        if j < NQ and ahead:
                            turn_high(m, 1 - u, j)
                        if j == 2:
                            act.wait_ge(gap_ready, n.lin(1, 1))
                            nc.scalar.activation(top[:, 3, :], top[:, 2, :], ACT.Exp).then_inc(ratio_ready, 1)
                    act.wait_ge(acc_full, n.lin(NA, NA))
                    nc.scalar.activation(hw[:, :], acc[(NA - 1) % 4][:, :], ACT.Copy).then_inc(acc_hi, 1)
                    use = NO * u + NO - 1
                    act.wait_ge(acc_free, n.lin(NA, NA + 4))
                    act.wait_ge(out_stored[use % 2], pair * (32 * NO) + (32 * (use // 2) + 32))
                    nc.scalar.activation(out_hi[use % 2][:, :], hw[:, :], ACT.Copy).then_inc(acc_hi, 1)
            over_chunks(act, pair_of_chunks)

        @block.vector
        def _(dve):
            def linker(sem_, start):
                done = [0]

                def link(ins):
                    done[0] += 1
                    ins.then_inc(sem_, 1)
                    dve.wait_ge(sem_, start(done[0]))
                return link, done

            def variances(m):
                link, done = linker(ln_link, lambda k: m.lin(NLN, k))
                for t in range(TPC):
                    dve.wait_ge(x_loaded[t], m.lin(16, 16))
                    for h in range(2):
                        ins = nc.vector.bn_stats(stats[:, t, h, :], x_sb[:, t, h * 512:(h + 1) * 512])
                link(ins)
                dve.sem_inc(passed, 1)
                for t in range(TPC):
                    ins = nc.vector.bn_aggr(mv[:, t, :], stats[:, t, :, :])
                link(ins)
                nc.vector.tensor_scalar(var[:, :], mv[:, :, 1], EPS, None, ALU.add).then_inc(var_ready, 1)

            def normalise(m):
                link, done = linker(ln_link, lambda k: m.lin(NLN, 2 + k))
                dve.wait_ge(std_ready, m.lin(1, 1))
                link(nc.vector.reciprocal(inv[:, 0, :], std[:, :]))
                link(nc.vector.tensor_mul(inv[:, 1, :], inv[:, 0, :], inv[:, 0, :]))
                link(nc.vector.tensor_mul(inv[:, 2, :], inv[:, 1, :], var[:, :]))
                link(nc.vector.tensor_scalar(inv[:, 1, :], inv[:, 2, :], -0.5, 1.5, ALU.mult, ALU.add))
                link(nc.vector.tensor_mul(inv[:, 3, :], inv[:, 0, :], inv[:, 1, :]))
                assert 2 + done[0] == NLN
                for t in range(TPC):
                    nc.vector.tensor_scalar(x_sb[:, t, :], x_sb[:, t, :], mv[:, t, 0:1], inv[:, 3, t:t + 1],
                                            ALU.subtract, ALU.mult).then_inc(xn_ready, 1)

            def turn_low(m, u, j):
                t, half = j // 2, j % 2
                dve.wait_ge(turn_hi, m.lin(NTR, j + 1))
                at = (slice(None), slice(half * 4, half * 4 + 4), slice(t * P, (t + 1) * P))
                nc.vector.tensor_sub(xt_lo[u][at], turned[j % 4][:, :].rearrange("p (k c) -> p k c", k=4),
                                     xt_hi[u][at].bitcast(FP32)).then_inc(turn_free, 1)

            dve.sem_inc(turn_free, 4)
            dve.sem_inc(acc_free, 4)
            zero = Step(0, 0)
            variances(zero)
            normalise(zero)
            for j in range(NTR):
                turn_low(zero, 0, j)
            for i in range(2 * KT):
                k, cols, slot, raw = w_piece(i)
                dve.wait_ge(w_hi_ready, i + 1)
                nc.vector.tensor_sub(w_lo[:, k, cols], raw, w_hi[:, k, cols].bitcast(FP32)).then_inc(w_lo_ready, 1)
            dve.wait_ge(rank_ready, 1)

            def winner(link, values, best, mask):
                link(nc.vector.tensor_reduce(best, values[:, :, :], AX.X, ALU.max))
                link(nc.vector.tensor_tensor(eq[:, :, :], values[:, :, :], bcast(best, 2, E), ALU.is_equal))
                link(nc.vector.tensor_mul(eq[:, :, :], eq[:, :, :], rank[:, :, :]))
                link(nc.vector.tensor_reduce(top[:, 4, :], eq[:, :, :], AX.X, ALU.max))
                link(nc.vector.tensor_tensor(mask[:, :, :], eq[:, :, :], bcast(top[:, 4, :], 2, E), ALU.is_equal))

            def pair_of_chunks(pair, b, last):
                for u in range(2):
                    n = Step(pair, u)
                    m = Step(pair, 1) if u == 0 else Step(pair + 1, 0)
                    ahead = not (last and u == 1)
                    if ahead:
                        variances(m)
                    for t in range(TPC):
                        dve.wait_ge(acc_hi, n.lin(NA, t + 1))
                        nc.vector.tensor_copy(logits[:, t, :], acc[t % 4][:, C_R:C_Q]).then_inc(acc_free, 1)
                    if ahead:
                        normalise(m)
                    link, done = linker(rt_link, lambda k: n.lin(NRT, k))
                    dve.wait_ge(acc_free, n.lin(NA, TPC + 4))
                    winner(link, logits, top[:, 0, :], first)
                    link(nc.vector.scalar_tensor_tensor(rest[:, :, :], first[:, :, :], MASKED, logits[:, :, :],
                                                        ALU.mult, ALU.add))
                    winner(link, rest, top[:, 1, :], second)
                    nc.vector.tensor_sub(top[:, 2, :], top[:, 1, :], top[:, 0, :]).then_inc(gap_ready, 1)
                    for j in range(NQ + NK):
                        item, use = TPC + j, NO * u + j
                        dve.wait_ge(acc_hi, n.lin(NA, item + 1))
                        nc.vector.scalar_tensor_tensor(out_lo[use % 2][:, :], acc[item % 4][:, :],
                                                       SCALE if j < NQ else 1.0, out_hi[use % 2][:, :].bitcast(FP32),
                                                       ALU.mult, ALU.subtract).then_inc(acc_free, 1)
                        if j < NQ and ahead:
                            turn_low(m, 1 - u, j)
                        if j == 3:
                            dve.wait_ge(ratio_ready, n.lin(1, 1))
                            link(nc.vector.tensor_scalar(top[:, 5, :], top[:, 3, :], 1.0, None, ALU.add))
                            link(nc.vector.reciprocal(top[:, 6, :], top[:, 5, :]))
                            link(nc.vector.tensor_scalar(top[:, 6, :], top[:, 6, :], LORA_SCALING, None, ALU.mult))
                            link(nc.vector.tensor_mul(top[:, 7, :], top[:, 6, :], top[:, 3, :]))
                            link(nc.vector.tensor_mul(first[:, :, :], first[:, :, :], bcast(top[:, 6, :], 2, E)))
                            link(nc.vector.tensor_mul(second[:, :, :], second[:, :, :], bcast(top[:, 7, :], 2, E)))
                            nc.vector.tensor_add(hw[:, :].rearrange("p (t e r) -> p t e r", t=TPC, e=E),
                                                 bcast(first[:, :, :], 3, R), bcast(second[:, :, :], 3, R)) \
                                .then_inc(route_ready, 1)
                            assert done[0] == NRT, done
                    dve.wait_ge(acc_hi, n.lin(NA, NA - 1))
                    nc.vector.tensor_mul(hw[:, :], acc[(NA - 2) % 4][:, :], hw[:, :]).then_inc(acc_free, 2)
                    dve.wait_ge(acc_hi, n.lin(NA, NA))
                    use = NO * u + NO - 1
                    nc.vector.tensor_sub(out_lo[use % 2][:, :], hw[:, :], out_hi[use % 2][:, :].bitcast(FP32)) \
                        .then_inc(hw_lo_ready, 1)
            over_chunks(dve, pair_of_chunks)

        @block.tensor
        def _(pe):
            def turn(m, j):
                t, half = j // 2, j % 2
                pe.wait_ge(xn_ready, m.lin(TPC, t + 1))
                pe.wait_ge(turn_free, m.lin(NTR, j + 1))
                for i in range(4):
                    k = half * 4 + i
                    ins = nc.tensor.transpose(turned[j % 4][:, i * P:(i + 1) * P], x_sb[:, t, k * P:(k + 1) * P], ident[:, :])
                ins.then_inc(turn_full, 1)

            def product(out, lhs, rhs):
                for k in range(KT):
                    (lh, ll), (rh, rl) = lhs(k), rhs(k)
                    nc.tensor.matmul(out, lh, rh, start=(k == 0), stop=False)
                    nc.tensor.matmul(out, lh, rl, start=False, stop=False)
                    ins = nc.tensor.matmul(out, ll, rh, start=False, stop=(k == KT - 1))
                return ins

            zero = Step(0, 0)
            for j in range(NTR):
                turn(zero, j)
            pe.wait_ge(w_lo_ready, KT)

            def pair_of_chunks(pair, b, last):
                for u in range(2):
                    n = Step(pair, u)
                    m = Step(pair, 1) if u == 0 else Step(pair + 1, 0)
                    ahead = not (last and u == 1)

                    def weights(k, c0, c1):
                        return w_hi[:, k, c0:c1], w_lo[:, k, c0:c1]

                    def tokens(k, c0=0, c1=CH):
                        return xt_hi[u][:, k, c0:c1], xt_lo[u][:, k, c0:c1]

                    pe.wait_ge(turn_free, n.lin(NTR, NTR + 4))
                    for t in range(TPC):
                        pe.wait_ge(acc_free, n.lin(NA, t + 1))
                        product(acc[t % 4][:, C_V:C_Q], lambda k: tokens(k, t * P, (t + 1) * P),
                                lambda k: weights(k, C_V, C_Q)).then_inc(acc_full, 1)
                    for j in range(NQ + NK + 1):
                        item = TPC + j
                        c0 = C_Q + j * P
                        if c0 == C_SPLIT:
                            pe.wait_ge(w_lo_ready, 2 * KT)
                        pe.wait_ge(acc_free, n.lin(NA, item + 1))
                        product(acc[item % 4][:, :], lambda k: weights(k, c0, c0 + P), tokens).then_inc(acc_full, 1)
                        if j < NQ and ahead:
                            turn(m, j)
                    pe.wait_ge(route_ready, n.lin(1, 1))
                    pe.wait_ge(acc_free, n.lin(NA, NA))
                    for t in range(TPC):
                        ins = nc.tensor.matmul(acc[(NA - 1) % 4][:, t * P:(t + 1) * P], hw[:, t * P:(t + 1) * P],
                                               ident[:, :], start=True, stop=True)
                    ins.then_inc(acc_full, 1)
            over_chunks(pe, pair_of_chunks)


def pieces_of(c):
    return [(i, h, p, min(CH, (TPC * c + i + 1) * P - CH * p))
            for i in range(TPC) for h in range(NREP) for p in range(c + 1)]


PIECES = [(c, n == len(pieces_of(c)) - 1, piece) for c in range(CPB) for n, piece in enumerate(pieces_of(c))]
NPG = len(PIECES)
T_OFF = [NREP * TPC * c * (c + 1) // 2 for c in range(CPB + 1)]
J_OFF = [t // NREP for t in T_OFF]
NTG, NJG = T_OFF[CPB], J_OFF[CPB]
assert NPG == NTG
LEAD = 72
TURN_AFTER = 2
NROWS, NCOLS = 4, 2
NSLICE = 8


def piece_at(i):
    return (i // NPG, *PIECES[i % NPG])


def stage(c):
    steps, old = TPC * (c + 1), TPC * ((c - 1) % CPB + 1)
    order = []
    for j in range(steps):
        for h in range(NREP):
            t = T_OFF[c] + NREP * j + h
            order.append(("T", j, h))
            order.append(("S", *piece_at(t + LEAD)))
            turned = piece_at(t + LEAD - TURN_AFTER)
            if turned[2]:
                order.append(("M", turned[0], turned[1]))
            if j == 0 and h == 1:
                order += [("V", old - 2, "before"), ("L", old - 2, "before")]
            if j == 0 and h == 3:
                order += [("V", old - 1, "before"), ("L", old - 1, "before"), ("Y", "before")]
            if j == 1 and h == 1:
                order.append(("O",))
            slot = (NREP * (j - 2) + h) // (1 if c == 0 else 2)
            if 0 <= slot < NSLICE and (c == 0 or h % 2):
                order.append(("I", slot))
            if j >= 2 and h == 1:
                order.append(("V", j - 2))
            if j >= 2 and h == 3:
                order.append(("L", j - 2))
        if j == (3 if c == 0 else 5):
            order.append(("N",))
    return order


STAGES = [stage(c) for c in range(CPB)]


def before(op):
    return op[0] in ("O", "I", "N") or op[-1] == "before"


def first_uses():
    out = []
    for i in range(LEAD):
        out.append(("S", *piece_at(i)))
        if i >= TURN_AFTER and piece_at(i - TURN_AFTER)[2]:
            out.append(("M", *piece_at(i - TURN_AFTER)[:2]))
    return out


FIRST_USES = first_uses()
USES = [sum(op[0] in "SM" for op in st) for st in STAGES]
NSG = sum(USES)
S_OFF = [len(FIRST_USES) + sum(USES[:c]) for c in range(CPB)]
assert NSG % NROWS == 0
ADDS = {"pool": [[], [0, 1, 3, 4, 6], [0, 1, 3, 4, 6, 7, 9, 10], [0, 1, 3, 4, 6, 7, 9, 10, 12, 13]]}


def adds_through(who, c, j):
    return sum(max(0, len(a) - 1) for a in ADDS[who][:c]) + sum(1 for t in ADDS[who][c][1:] if t <= j)


def adds_of_group(who):
    return adds_through(who, CPB - 1, NJG)


def attend(nc, sc, ident, ident_b, mask_ij, mask_ji, wb, lb, gw_hi, gw_lo):
    ctx = ExitStack()
    with ctx:
        def sb(name, shape, dt=FP32):
            return ctx.enter_context(nc.sbuf_tensor(name, shape, dt))

        def sem(name):
            return ctx.enter_context(nc.semaphore(name))

        K1 = 3 * HD
        q_st = [sb(f"q_st{i}", [K1 + 1, NREP, CH], FP32R) for i in range(CPB)]
        k_st = [sb(f"k_st{i}", [K1 + 1, S], FP32R) for i in range(2)]
        v_st = [sb(f"v_st{i}", [P, S // P, HD]) for i in range(2)]
        ones = sb("ones", [P, HD])
        probs = [sb(f"probs{i}", [P, NREP, CH]) for i in range(4)]
        added = {who: sb(f"added_{who}", [P, NREP, CH]) for who in ADDS}
        neg_max = [sb(f"neg_max{i}", [P, NREP * TPC, CPB]) for i in range(2)]
        shift = sb("shift", [P, 16], FP32R)
        row = [sb(f"row{i}", [16, P]) for i in range(2)]
        o_raw = [sb(f"a_o_raw{i}", [P, CH]) for i in range(2)]
        l_raw = [sb(f"l_raw{i}", [P, CH]) for i in range(2)]
        o_sb = [sb(f"o_sb{i}", [P, CH]) for i in range(2)]
        gw_raw = sb("gw_raw", [P, 4, D])
        rows_ps = [ctx.enter_context(nc.psum_tensor(f"rows_ps{i}", [P, CH], FP32)) for i in range(NROWS)]
        cols_ps = [ctx.enter_context(nc.psum_tensor(f"cols_ps{i}", [P, CH], FP32)) for i in range(NCOLS)]
        o_ps = ctx.enter_context(nc.psum_tensor("o_ps", [P, CH], FP32))
        l_ps = ctx.enter_context(nc.psum_tensor("l_ps", [P, CH], FP32))

        passed = sem("a_passed")
        q_loaded = [sem(f"a_q_loaded{i}") for i in range(CPB)]
        k_loaded = [sem(f"a_k_loaded{i}") for i in range(2)]
        v_loaded = [sem(f"a_v_loaded{i}") for i in range(2)]
        ones_ready = sem("a_ones_ready")
        rows_full = sem("a_rows_full")
        rows_free = sem("a_rows_free")
        shift_ready = sem("a_shift_ready")
        row_moved = [sem(f"a_row_moved{i}") for i in range(2)]
        cols_full = sem("a_cols_full")
        probs_ready = sem("a_probs_ready")
        values_done = sem("a_values_done")
        pool_added = sem("a_pool_added")
        add_done = {"pool": pool_added}
        chunk_full = sem("a_chunk_full")
        chunk_copied = sem("a_chunk_copied")
        inv_link = sem("a_inv_link")
        o_ready = sem("a_o_ready")
        o_stored = [sem(f"a_o_stored{i}") for i in range(2)]

        gw_loaded = [sem(f"a_gw_loaded{i}") for i in range(4)]
        gw_hi_ready = sem("a_gw_hi_ready")
        gw_lo_ready = sem("a_gw_lo_ready")
        NW = KT + 1

        block = ctx.enter_context(nc.Block())
        NPAIR = NG // 2

        def over_stages(engine, run):
            run(Step(0, 0), 0, 0, [op for op in STAGES[0] if not before(op)])
            with engine.Fori(0, NPAIR - 1) as pair:
                for c in range(1, CPB):
                    run(Step(pair, 0), 0, c, STAGES[c])
                for c in range(CPB):
                    run(Step(pair, 1), 1, c, STAGES[c])
                run(Step(pair + 1, 0), 0, 0, STAGES[0])
            last = NPAIR - 1
            for c in range(1, CPB):
                run(Step(last, 0), 0, c, STAGES[c])
            for c in range(CPB):
                run(Step(last, 1), 1, c, [op for op in STAGES[c] if op[0] not in "SM" or op[1] == 0])
            run(Step(NPAIR, 0), 0, 0, [op for op in STAGES[0] if before(op)])

        @block.sync
        def _(sp):
            def load_q(n, c):
                for i, part in enumerate(("hi", "lo", "hi")):
                    src = sc["q_" + part].rearrange("b g (h d) c -> (b g) d h c", d=HD)
                    sp.dma_start(q_st[c][i * HD:(i + 1) * HD, :, :].bitcast(FP32),
                                 src[bass.ds(n, 1), :, :, c * CH:(c + 1) * CH].squeeze(0)).then_inc(q_loaded[c], 16)

            def load_kv(n, u):
                for i, part in enumerate(("hi", "hi", "lo")):
                    src = sc["k_" + part].rearrange("b g d c -> (b g) d c")
                    sp.dma_start(k_st[u][i * HD:(i + 1) * HD, :].bitcast(FP32), src[bass.ds(n, 1), :, :].squeeze(0)) \
                      .then_inc(k_loaded[u], 16)
                src = sc["v"].rearrange("b g p c -> (b g) p c")
                sp.dma_start(v_st[u][:, :, :].rearrange("p j d -> p (j d)"), src[bass.ds(n, 1), :, :].squeeze(0)) \
                  .then_inc(v_loaded[u], 16)

            def move_row(free, c):
                sp.wait_ge(rows_free, free)
                sp.dma_start(q_st[c][K1:K1 + 1, :, :].bitcast(FP32), row[c % 2][:, :]).then_inc(row_moved[c % 2], 16)

            for s in o_stored:
                sp.sem_inc(s, 16)
            load_kv(0, 0)
            load_q(0, 0)
            load_q(0, 1)
            load_q(0, 2)
            for use, op in enumerate(FIRST_USES):
                if op[0] == "M":
                    move_row(NROWS + use + 1, op[2])

            def run(n, u, c, ops):
                last_group = isinstance(n.pair, int) and n.pair == NPAIR - 1 and u == 1
                use = 0
                for op in ops:
                    kind = op[0]
                    if kind == "T" and op[1:] == (0, 0):
                        if c == 0 or not last_group:
                            wait_apart(sp, values_done, n.lin(NJG, J_OFF[c] + 4), passed)
                            load_q(n.lin(1, 0 if c == 0 else 1), (c - 1) % CPB)
                        if c == 0 and not last_group:
                            load_kv(n.lin(1, 1), 1 - u)
                    elif kind == "M":
                        move_row(n.lin(NSG, NROWS + S_OFF[c] + use + 1), op[2])
                    elif kind == "N":
                        wait_apart(sp, o_ready, n.lin(CPB, c + 2), passed)
                        dst = sc["o"].rearrange("b g p c -> (b g) p c")
                        cp = (c - 1) % CPB
                        sp.dma_start(dst[bass.ds(n.lin(1, -1 if c == 0 else 0), 1), :, cp * CH:(cp + 1) * CH].squeeze(0),
                                     o_sb[cp % 2][:, :]).then_inc(o_stored[cp % 2], 16)
                    if kind in "SM":
                        use += 1
            over_stages(sp, run)
            for s in range(2):
                sp.wait_ge(o_stored[s], 16 + 16 * (CPB * NG // 2))

        @block.gpsimd
        def _(pool):
            pool.sem_inc(pool_added, 1)
            for k in range(NW):
                pool.wait_ge(gw_hi_ready, k + 1)
                nc.gpsimd.tensor_tensor(gw_lo[:, k, :], gw_raw[:, k % 4, :], gw_hi[:, k, :].bitcast(FP32), ALU.subtract) \
                    .then_inc(gw_lo_ready, 1)

            def run(n, u, c, ops):
                mine = ADDS["pool"][c]
                if not any(op[0] == "T" for op in ops):
                    return
                for first, j in zip([True] + [False] * NJG, mine[1:]):
                    q0 = max(0, j - TPC * c) * P
                    pool.wait_ge(probs_ready, n.lin(NTG, T_OFF[c] + NREP * (j + 1) + NCOLS))
                    if first:
                        pool.wait_ge(chunk_full, n.lin(CPB - 1, c))
                        a = probs[mine[0] % 4]
                    else:
                        pool.wait_ge(pool_added, n.lin(adds_of_group("pool"), adds_through("pool", c, j)))
                        a = added["pool"]
                    nc.gpsimd.tensor_tensor(added["pool"][:, :, q0:CH], a[:, :, q0:CH], probs[j % 4][:, :, q0:CH],
                                            ALU.add).then_inc(pool_added, 1)
            over_stages(pool, run)

        @block.tensor
        def _(pe):
            def row_scores(value, bank, kbuf, c, i, h, p, keys):
                pe.wait_ge(rows_free, value + 1)
                out = rows_ps[bank % NROWS]
                ins = nc.tensor.matmul(out[:, 0:keys], q_st[c][0:K1, h, i * P:(i + 1) * P],
                                       k_st[kbuf][0:K1, CH * p:CH * p + keys], start=True, stop=p < c)
                if p == c:
                    ins = nc.tensor.matmul(out[:, keys - P:keys], ident_b[:, :], mask_ij[:, :], start=False, stop=True)
                ins.then_inc(rows_full, 1)

            def turn_shift(value, bank, chunk_count):
                pe.wait_ge(shift_ready, chunk_count)
                pe.wait_ge(rows_free, value + 1)
                nc.tensor.transpose(rows_ps[bank % NROWS][0:16, 0:P], shift[:, :].bitcast(FP32), ident[:, :]) \
                    .then_inc(rows_full, 1)

            pe.sem_inc(values_done, 4)
            pe.sem_inc(chunk_full, 1)
            pe.wait_ge(ones_ready, 1)
            pe.wait_ge(q_loaded[0], 48)
            pe.wait_ge(k_loaded[0], 48)
            for use, op in enumerate(FIRST_USES):
                if op[0] == "S":
                    if op[4] == pieces_of(op[2])[0]:
                        pe.wait_ge(q_loaded[op[2]], 48)
                    row_scores(use, use, 0, op[2], *op[4])
                else:
                    turn_shift(use, use, op[2] + 1)

            def run(n, u, c, ops):
                use = 0
                for op in ops:
                    kind = op[0]
                    if kind in "VLY":
                        old = op[-1] == "before"
                        cc = (c - 1) % CPB if old else c
                        back = 1 if old and c == 0 else 0
                        steps = TPC * (cc + 1)
                        to_sum = [j for j in range(steps) if not any(j in ADDS[who][cc] for who in ADDS)]
                        adders = [who for who in ADDS if ADDS[who][cc]]
                    if kind == "S":
                        ahead, chunk, _, piece = op[1:]
                        if piece == pieces_of(chunk)[0]:
                            pe.wait_ge(q_loaded[chunk], n.lin(48, 48 * (1 + ahead)))
                            if chunk == 0:
                                pe.wait_ge(k_loaded[(u + ahead) % 2], n.pair * 48 + 48 * (1 + (u + ahead) // 2))
                        row_scores(n.lin(NSG, S_OFF[c] + use), S_OFF[c] + use, (u + ahead) % 2, chunk, *piece)
                        use += 1
                    elif kind == "M":
                        turn_shift(n.lin(NSG, S_OFF[c] + use), S_OFF[c] + use, n.lin(CPB, CPB * op[1] + op[2] + 1))
                        use += 1
                    elif kind == "T":
                        j, h = op[1:]
                        q0 = max(0, j - TPC * c) * P
                        if j == 0 and h == 0:
                            pe.wait_ge(row_moved[c % 2], n.lin(32, 16 * (c // 2 + 1)))
                        pe.wait_ge(probs_ready, n.lin(NTG, T_OFF[c] + NREP * j + h + 1))
                        diagonal = j >= TPC * c
                        ins = nc.tensor.matmul(cols_ps[h % NCOLS][:, q0:CH], k_st[u][:, j * P:(j + 1) * P], q_st[c][:, h, q0:CH],
                                               start=True, stop=not diagonal)
                        if diagonal:
                            ins = nc.tensor.matmul(cols_ps[h % NCOLS][:, q0:q0 + P], ident_b[:, :], mask_ji[:, :],
                                                   start=False, stop=True)
                        ins.then_inc(cols_full, 1)
                    elif kind == "V":
                        j = op[1]
                        q0 = max(0, j - TPC * cc) * P
                        vbuf = 1 - u if back else u
                        if j == 0:
                            pe.wait_ge(chunk_copied, n.lin(CPB, c + 1))
                            if c == 0:
                                pe.wait_ge(v_loaded[u], n.pair * 16 + 16)
                        pe.wait_ge(probs_ready, n.lin(NTG, T_OFF[cc] + NREP * (j + 1) + NCOLS - back * NTG))
                        for h in range(NREP):
                            ins = nc.tensor.matmul(o_ps[h * HD:(h + 1) * HD, q0:CH], v_st[vbuf][:, j, :],
                                                   probs[j % 4][:, h, q0:CH], start=(j == 0), stop=(j == steps - 1),
                                                   tile_position=(0, h * HD))
                        if j not in to_sum:
                            ins.then_inc(values_done, 1)
                    elif kind == "L":
                        j = op[1]
                        q0 = max(0, j - TPC * cc) * P
                        if j in to_sum:
                            for h in range(NREP):
                                ins = nc.tensor.matmul(l_ps[h * HD:(h + 1) * HD, q0:CH], ones[:, :],
                                                       probs[j % 4][:, h, q0:CH], start=(j == to_sum[0]),
                                                       stop=(j == to_sum[-1] and not adders), tile_position=(0, h * HD))
                            ins.then_inc(values_done, 1)
                    elif kind == "Y":
                        for who in adders:
                            pe.wait_ge(add_done[who], n.lin(adds_of_group(who), adds_through(who, cc, NJG) + 1
                                                            - back * adds_of_group(who)))
                            for h in range(NREP):
                                ins = nc.tensor.matmul(l_ps[h * HD:(h + 1) * HD, :], ones[:, :], added[who][:, h, :],
                                                       start=False, stop=(who == adders[-1]), tile_position=(0, h * HD))
                        if adders:
                            ins.then_inc(chunk_full, 1)
            over_stages(pe, run)

        @block.scalar
        def _(act):
            def load_gw(k):
                act.dma_start(gw_raw[:, k % 4, :], wb[k * P:(k + 1) * P, :] if k < KT else lb[:, :]) \
                   .then_inc(gw_loaded[k % 4], 16)

            act.sem_inc(probs_ready, NCOLS)
            act.sem_inc(chunk_copied, 1)
            act.wait_ge(k_loaded[0], 48)
            act.wait_ge(q_loaded[0], 48)
            for k in range(4):
                load_gw(k)
            for k in range(NW):
                act.wait_ge(gw_loaded[k % 4], 16 * (k // 4 + 1))
                nc.scalar.activation(gw_hi[:, k, :], gw_raw[:, k % 4, :], ACT.Copy).then_inc(gw_hi_ready, 1)
                if k >= 1 and k + 3 < NW:
                    act.wait_ge(gw_lo_ready, k)
                    load_gw(k + 3)

            def run(n, u, c, ops):
                cp, back = (c - 1) % CPB, 1 if c == 0 else 0
                for op in ops:
                    kind = op[0]
                    if kind == "T":
                        j, h = op[1:]
                        q0 = max(0, j - TPC * c) * P
                        act.wait_ge(cols_full, n.lin(NTG, T_OFF[c] + NREP * j + h + 1))
                        if h == 0:
                            act.wait_ge(values_done, n.lin(NJG, J_OFF[c] + j + 1))
                            c4, j4 = (c, j - 4) if j >= 4 else (cp, TPC * (cp + 1) + j - 4)
                            for who in ADDS:
                                if j4 in ADDS[who][c4] and not (n.pair == 0 and u == 0 and c == 0 if
                                                                isinstance(n.pair, int) else False):
                                    group = back if j < 4 else 0
                                    act.wait_ge(add_done[who], n.lin(
                                        adds_of_group(who), max(adds_through(who, c4, j4), adds_through(who, c4, ADDS[who][c4][1]))
                                        + 1 - group * adds_of_group(who)))
                        nc.scalar.activation(probs[j % 4][:, h, q0:CH], cols_ps[h % NCOLS][:, q0:CH], ACT.Exp) \
                            .then_inc(probs_ready, 1)
                    elif kind == "O":
                        if cp == 0:
                            act.wait_ge(values_done, n.lin(NJG, J_OFF[0] + TPC + 4))
                        else:
                            act.wait_ge(chunk_full, n.lin(CPB - 1, 1 if c == 0 else cp + 1))
                        act.wait_ge(o_ready, n.lin(CPB, c))
                        nc.scalar.activation(l_raw[cp % 2][:, :], l_ps[:, :], ACT.Copy)
                        nc.scalar.activation(o_raw[cp % 2][:, :], o_ps[:, :], ACT.Copy).then_inc(chunk_copied, 1)
            over_stages(act, run)

        @block.vector
        def _(dve):
            def piece_max(full, bank, chunk, i, h, p, keys):
                dve.wait_ge(rows_full, full)
                r = h * TPC + i
                nc.vector.tensor_reduce(neg_max[chunk % 2][:, r, p:p + 1], rows_ps[bank % NROWS][:, 0:keys], AX.X, ALU.max,
                                        negate=True).then_inc(rows_free, 1)

            def shifts(chunk, free):
                dve.wait_ge(rows_free, free)
                nc.vector.tensor_reduce(shift[:, :], neg_max[chunk % 2][:, :, 0:chunk + 1], AX.X, ALU.min).then_inc(shift_ready, 1)

            def row_out(full, bank, par):
                dve.wait_ge(rows_full, full)
                nc.vector.tensor_copy(row[par][:, :], rows_ps[bank % NROWS][0:16, 0:P]).then_inc(rows_free, 1)

            nc.vector.memset(ones[:, :], 1.0)
            for i in range(2):
                ins = nc.vector.memset(k_st[i][K1:K1 + 1, :].bitcast(FP32), 1.0)
            ins.then_inc(ones_ready, 1)
            dve.sem_inc(rows_free, NROWS)
            dve.sem_inc(o_ready, 2)
            for use, op in enumerate(FIRST_USES):
                if op[0] == "S":
                    piece_max(use + 1, use, op[2], *op[4])
                    if op[3]:
                        shifts(op[2], use + 1 + NROWS)
                else:
                    row_out(use + 1, use, op[2] % 2)

            def run(n, u, c, ops):
                cp = (c - 1) % CPB
                use = 0
                for op in ops:
                    kind = op[0]
                    at = S_OFF[c] + use
                    if kind == "S":
                        piece_max(n.lin(NSG, at + 1), at, op[2], *op[4])
                        if op[3]:
                            shifts(op[2], n.lin(NSG, at + 1 + NROWS))
                        use += 1
                    elif kind == "M":
                        row_out(n.lin(NSG, at + 1), at, op[2] % 2)
                        use += 1
                    elif kind == "I":
                        part = slice(op[1] * (CH // NSLICE), (op[1] + 1) * (CH // NSLICE))
                        if op[1] == 0:
                            dve.wait_ge(chunk_copied, n.lin(CPB, c + 1))
                        ins = nc.vector.reciprocal(l_raw[cp % 2][:, part], l_raw[cp % 2][:, part])
                        if op[1] == NSLICE - 1:
                            ins.then_inc(inv_link, 1)
                    elif kind == "N":
                        dve.wait_ge(inv_link, n.lin(CPB, c))
                        dve.wait_ge(o_stored[cp % 2], n.lin(32, 16 * ((c - 1) // 2) + 16))
                        nc.vector.tensor_mul(o_sb[cp % 2][:, :], o_raw[cp % 2][:, :], l_raw[cp % 2][:, :]).then_inc(o_ready, 1)
            over_stages(dve, run)


def gate(nc, b_base, sc, w_hi, w_lo, wo, ow_hi, ow_lo):
    ctx = ExitStack()
    with ctx:
        def sb(name, shape, dt=FP32):
            return ctx.enter_context(nc.sbuf_tensor(name, shape, dt))

        def sem(name):
            return ctx.enter_context(nc.semaphore(name))

        NW = KT + 1
        HALF = D // 2
        ow_raw = sb("ow_raw", [P, 2, D])
        bias = sb("g_bias", [P, D])
        t_hi = [sb(f"g_t_hi{i}", [P, NW, P], FP32R) for i in range(2)]
        t_lo = [sb(f"g_t_lo{i}", [P, NW, P], FP32R) for i in range(2)]
        z = sb("g_z", [P, 2, HALF])
        th = sb("g_th", [P, 2, HALF])
        g = sb("g_g", [P, 2, HALF])
        acc = [ctx.enter_context(nc.psum_tensor(f"g_acc{i}", [P, HALF], FP32)) for i in range(2)]
        passed = sem("g_passed")
        ow_loaded = [sem(f"g_ow_loaded{i}") for i in range(2)]
        bias_loaded = sem("g_bias_loaded")
        ow_hi_ready = sem("g_ow_hi_ready")
        ow_lo_ready = sem("g_ow_lo_ready")
        t_loaded = [sem(f"g_t_loaded{i}") for i in range(2)]
        acc_full = sem("g_acc_full")
        z_ready = sem("g_z_ready")
        th_ready = sem("g_th_ready")
        g_ready = sem("g_g_ready")
        g_stored = [sem(f"g_g_stored{i}") for i in range(2)]
        block = ctx.enter_context(nc.Block())
        NPAIR = NT // 2

        @block.sync
        def _(sp):
            for s in g_stored:
                sp.sem_inc(s, 16)
            sp.dma_start(bias[:, :], b_base.partition_broadcast(P)).then_inc(bias_loaded, 16)

            def load(i, u):
                for part, dst in (("hi", t_hi[u]), ("lo", t_lo[u])):
                    sp.dma_start(dst[:, 0:KT, :].bitcast(FP32), sc["xt_" + part][:, bass.ds(i, 1), :, :].squeeze(1)) \
                      .then_inc(t_loaded[u], 16)
                    sp.dma_start(dst[:, KT, :].bitcast(FP32), sc["hw_" + part][:, bass.ds(i * P, P)]) \
                      .then_inc(t_loaded[u], 16)

            def pair_of_tiles(pair, last):
                for u in range(2):
                    n = Step(pair, u)
                    for half in range(2):
                        wait_apart(sp, g_ready, n.lin(2, half + 1), passed)
                        sp.dma_start(sc["g"][bass.ds(n.lin(P), P), half * HALF:(half + 1) * HALF], g[:, half, :]) \
                          .then_inc(g_stored[half], 16)
                    if not last:
                        load(n.lin(1, 2), u)
            load(0, 0)
            load(1, 1)
            with sp.Fori(0, NPAIR - 1) as pair:
                pair_of_tiles(pair, False)
            pair_of_tiles(NPAIR - 1, True)
            for s in g_stored:
                sp.wait_ge(s, 16 * (NT + 1))

        @block.scalar
        def _(act):
            def load_ow(k):
                act.dma_start(ow_raw[:, k % 2, :], wo[k * P:(k + 1) * P, :]).then_inc(ow_loaded[k % 2], 16)

            def tanhs(n):
                for half in range(2):
                    act.wait_ge(z_ready, n.lin(2, half + 3))
                    nc.scalar.activation(th[:, half, :], z[:, half, :], ACT.Tanh, scale=0.5).then_inc(th_ready, 1)

            act.wait_ge(t_loaded[0], 64)
            load_ow(0)
            load_ow(1)
            for k in range(KT):
                tanhs(Step(k // 2, k % 2))
                act.wait_ge(ow_loaded[k % 2], 16 * (k // 2 + 1))
                nc.scalar.activation(ow_hi[:, k, :], ow_raw[:, k % 2, :], ACT.Copy).then_inc(ow_hi_ready, 1)
                if 1 <= k < KT - 1:
                    act.wait_ge(ow_lo_ready, k)
                    load_ow(k + 1)
            with act.Fori(KT // 2, NPAIR) as pair:
                for u in range(2):
                    tanhs(Step(pair, u))

        @block.vector
        def _(dve):
            def silu(n):
                for half in range(2):
                    dve.wait_ge(acc_full, n.lin(2, half + 1))
                    nc.vector.tensor_add(z[:, half, :], acc[half][:, :], bias[:, half * HALF:(half + 1) * HALF]) \
                        .then_inc(z_ready, 1)
                    dve.wait_ge(th_ready, n.lin(2, half + 1))
                    dve.wait_ge(g_stored[half], n.lin(16, 16))
                    nc.vector.scalar_tensor_tensor(g[:, half, :], th[:, half, :], 1.0, z[:, half, :], ALU.add, ALU.mult) \
                        .then_inc(g_ready, 1)

            dve.sem_inc(z_ready, 2)
            dve.wait_ge(bias_loaded, 16)
            for k in range(KT):
                silu(Step(k // 2, k % 2))
                dve.wait_ge(ow_hi_ready, k + 1)
                nc.vector.tensor_sub(ow_lo[:, k, :], ow_raw[:, k % 2, :], ow_hi[:, k, :].bitcast(FP32)) \
                    .then_inc(ow_lo_ready, 1)
            with dve.Fori(KT // 2, NPAIR) as pair:
                for u in range(2):
                    silu(Step(pair, u))

        @block.tensor
        def _(pe):
            with pe.Fori(0, NPAIR) as pair:
                for u in range(2):
                    n = Step(pair, u)
                    pe.wait_ge(t_loaded[u], pair * 64 + 64)
                    for half in range(2):
                        pe.wait_ge(z_ready, n.lin(2, half + 1))
                        cols = slice(half * HALF, (half + 1) * HALF)
                        for k in range(NW):
                            nc.tensor.matmul(acc[half][:, :], t_hi[u][:, k, :], w_hi[:, k, cols], start=(k == 0), stop=False)
                            nc.tensor.matmul(acc[half][:, :], t_hi[u][:, k, :], w_lo[:, k, cols], start=False, stop=False)
                            ins = nc.tensor.matmul(acc[half][:, :], t_lo[u][:, k, :], w_hi[:, k, cols], start=False,
                                                   stop=(k == NW - 1))
                        ins.then_inc(acc_full, 1)


def output(nc, x, sc, out, w_hi, w_lo):
    ctx = ExitStack()
    with ctx:
        def sb(name, shape, dt=FP32):
            return ctx.enter_context(nc.sbuf_tensor(name, shape, dt))

        def sem(name):
            return ctx.enter_context(nc.semaphore(name))

        HALF = D // 2
        o_raw = [sb(f"o_raw{i}", [P, KT, P]) for i in range(2)]
        t_hi = [sb(f"o_t_hi{i}", [P, KT, P], FP32R) for i in range(2)]
        t_lo = [sb(f"o_t_lo{i}", [P, KT, P], FP32R) for i in range(2)]
        x_sb = sb("o_x", [P, 2, D])
        g_sb = sb("o_g", [P, 2, D])
        prod = sb("o_prod", [P, 2, HALF])
        y = sb("o_y", [P, 2, HALF])
        acc = [ctx.enter_context(nc.psum_tensor(f"o_acc{i}", [P, HALF], FP32)) for i in range(2)]
        passed = sem("o_passed")
        t_loaded = [sem(f"o_t_loaded{i}") for i in range(2)]
        xg_loaded = [sem(f"o_xg_loaded{i}") for i in range(2)]
        t_hi_ready = sem("o_t_hi_ready")
        t_lo_ready = sem("o_t_lo_ready")
        acc_full = sem("o_acc_full")
        prod_ready = sem("o_prod_ready")
        y_ready = sem("o_y_ready")
        y_stored = [sem(f"o_y_stored{i}") for i in range(2)]
        block = ctx.enter_context(nc.Block())
        NPAIR = NT // 2
        o_src = sc["o"].rearrange("b g p c -> p b g c")

        @block.sync
        def _(sp):
            for s in y_stored:
                sp.sem_inc(s, 16)

            def load(i, b, u):
                sp.dma_start(o_raw[u][:, :, :], o_src[:, b, :, bass.ds(i * P - b * S, P)]).then_inc(t_loaded[u], 16)
                sp.dma_start(x_sb[:, u, :], x[bass.ds(i * P, P), :]).then_inc(xg_loaded[u], 16)
                sp.dma_start(g_sb[:, u, :], sc["g"][bass.ds(i * P, P), :]).then_inc(xg_loaded[u], 16)

            def pair_of_tiles(pair, b, last):
                for u in range(2):
                    n = Step(pair, u)
                    for half in range(2):
                        wait_apart(sp, y_ready, n.lin(2, half + 1), passed)
                        sp.dma_start(out[bass.ds(n.lin(P), P), half * HALF:(half + 1) * HALF], y[:, half, :]) \
                          .then_inc(y_stored[half], 16)
                    if not last:
                        load(n.lin(1, 2), b, u)
            load(0, 0, 0)
            load(1, 0, 1)
            with sp.Fori(0, NPAIR // 2 - 1) as pair:
                pair_of_tiles(pair, 0, False)
            with sp.Fori(NPAIR // 2 - 1, NPAIR - 1) as pair:
                pair_of_tiles(pair, 1, False)
            pair_of_tiles(NPAIR - 1, 1, True)
            for s in y_stored:
                sp.wait_ge(s, 16 * (NT + 1))

        @block.scalar
        def _(act):
            def high(n, u):
                act.wait_ge(t_loaded[u], n.pair * 16 + 16)
                nc.scalar.activation(t_hi[u][:, :, :], o_raw[u][:, :, :], ACT.Copy).then_inc(t_hi_ready, 1)
            high(Step(0, 0), 0)
            high(Step(0, 1), 1)
            with act.Fori(0, NPAIR - 1) as pair:
                for u in range(2):
                    act.wait_ge(acc_full, Step(pair, u).lin(2, 2))
                    high(Step(pair + 1, u), u)

        @block.vector
        def _(dve):
            def low(n, u):
                dve.wait_ge(t_hi_ready, n.lin(1, 1))
                nc.vector.tensor_sub(t_lo[u][:, :, :], o_raw[u][:, :, :], t_hi[u][:, :, :].bitcast(FP32)) \
                    .then_inc(t_lo_ready, 1)

            def finish(n, u):
                for half in range(2):
                    cols = slice(half * HALF, (half + 1) * HALF)
                    dve.wait_ge(acc_full, n.lin(2, half + 1))
                    if half == 0:
                        dve.wait_ge(xg_loaded[u], n.pair * 32 + 32)
                    nc.vector.scalar_tensor_tensor(prod[:, half, :], acc[half][:, :], 0.5, g_sb[:, u, cols],
                                                   ALU.mult, ALU.mult).then_inc(prod_ready, 1)
                    dve.wait_ge(prod_ready, n.lin(2, half + 3))
                    dve.wait_ge(y_stored[half], n.lin(16, 16))
                    nc.vector.tensor_add(y[:, half, :], prod[:, half, :], x_sb[:, u, cols]).then_inc(y_ready, 1)
            dve.sem_inc(prod_ready, 2)
            low(Step(0, 0), 0)
            low(Step(0, 1), 1)
            with dve.Fori(0, NPAIR - 1) as pair:
                for u in range(2):
                    finish(Step(pair, u), u)
                    low(Step(pair + 1, u), u)
            for u in range(2):
                finish(Step(NPAIR - 1, u), u)

        @block.tensor
        def _(pe):
            with pe.Fori(0, NPAIR) as pair:
                for u in range(2):
                    n = Step(pair, u)
                    pe.wait_ge(t_lo_ready, n.lin(1, 1))
                    for half in range(2):
                        pe.wait_ge(prod_ready, n.lin(2, half + 1))
                        cols = slice(half * HALF, (half + 1) * HALF)
                        for k in range(KT):
                            nc.tensor.matmul(acc[half][:, :], t_hi[u][:, k, :], w_hi[:, k, cols], start=(k == 0), stop=False)
                            nc.tensor.matmul(acc[half][:, :], t_hi[u][:, k, :], w_lo[:, k, cols], start=False, stop=False)
                            ins = nc.tensor.matmul(acc[half][:, :], t_lo[u][:, k, :], w_hi[:, k, cols], start=False,
                                                   stop=(k == KT - 1))
                        ins.then_inc(acc_full, 1)


def program(nc, x, wall, wo, wb, b_base, lb, out):
    def scratch(name, *shape):
        return nc.dram_tensor("scratch_" + name, shape, FP32, kind="Internal").ap()

    sc = {}
    for part in ("hi", "lo"):
        sc["xt_" + part] = scratch("xt_" + part, P, NT, KT, P)
        sc["q_" + part] = scratch("q_" + part, B, NKV, P, S)
        sc["k_" + part] = scratch("k_" + part, B, NKV, HD, S)
        sc["hw_" + part] = scratch("hw_" + part, P, T)
    sc["v"] = scratch("v", B, NKV, P, S // P * HD)
    sc["o"] = scratch("o", B, NKV, P, S)
    sc["g"] = scratch("g", T, D)

    with ExitStack() as ctx:
        ident = ctx.enter_context(nc.sbuf_tensor("ident", [P, P], FP32))
        ident_b = ctx.enter_context(nc.sbuf_tensor("ident_b", [P, P], BF16))
        mask_ij = ctx.enter_context(nc.sbuf_tensor("mask_ij", [P, P], BF16))
        mask_ji = ctx.enter_context(nc.sbuf_tensor("mask_ji", [P, P], BF16))
        made = ctx.enter_context(nc.semaphore("made"))
        with nc.Block() as block:
            @block.gpsimd
            def _(pool):
                for m in (ident, ident_b, mask_ij, mask_ji):
                    nc.gpsimd.memset(m[:, :], 0.0).then_inc(made, 1)
                pool.wait_ge(made, 4)
                for m in (ident, ident_b):
                    nc.gpsimd.affine_select(out=m[:, :], in_=m[:, :], compare_op=ALU.not_equal, fill=1.0, base=0,
                                            pattern=[[-1, P]], channel_multiplier=1).then_inc(made, 1)
                nc.gpsimd.affine_select(out=mask_ij[:, :], in_=mask_ij[:, :], compare_op=ALU.is_ge, fill=MASKED, base=0,
                                        pattern=[[-1, P]], channel_multiplier=1).then_inc(made, 1)
                nc.gpsimd.affine_select(out=mask_ji[:, :], in_=mask_ji[:, :], compare_op=ALU.is_ge, fill=MASKED, base=0,
                                        pattern=[[1, P]], channel_multiplier=-1).then_inc(made, 1)
                pool.wait_ge(made, 8)
        project(nc, x, wall, sc, ident)
        gw_hi, gw_lo = (ctx.enter_context(nc.sbuf_tensor("gw_" + part, [P, KT + 1, D], FP32R)) for part in ("hi", "lo"))
        attend(nc, sc, ident, ident_b, mask_ij, mask_ji, wb, lb, gw_hi, gw_lo)
        ow_hi, ow_lo = (ctx.enter_context(nc.sbuf_tensor("ow_" + part, [P, KT, D], FP32R)) for part in ("hi", "lo"))
        gate(nc, b_base, sc, gw_hi, gw_lo, wo, ow_hi, ow_lo)
        output(nc, x, sc, out, ow_hi, ow_lo)


def kernel(L0_attn_x, L0_attn_wq, L0_attn_wk, L0_attn_wv, L0_attn_wo, L0_ffn_W_base, L0_ffn_b_base, L0_ffn_W_router,
           L0_ffn_lora_A, L0_ffn_lora_B):
    import numpy as np
    import concourse.bacc as bacc
    from concourse.bass_utils import run_bass_kernel_spmd

    arrays = {
        "x": np.ascontiguousarray(L0_attn_x).reshape(T, D),
        "wall": np.concatenate([np.asarray(L0_attn_wv), np.asarray(L0_ffn_W_router).T, np.asarray(L0_attn_wq),
                                np.asarray(L0_attn_wk), np.asarray(L0_ffn_lora_A).reshape(E * R, D).T], axis=1),
        "wo": np.ascontiguousarray(L0_attn_wo),
        "wb": np.ascontiguousarray(np.asarray(L0_ffn_W_base).T),
        "b_base": np.ascontiguousarray(L0_ffn_b_base),
        "lb": np.ascontiguousarray(np.asarray(L0_ffn_lora_B).transpose(0, 2, 1)).reshape(E * R, D),
    }
    nc = bacc.Bacc("TRN2", target_bir_lowering=False, num_devices=1)
    args = [nc.dram_tensor("in_" + k, a.shape, FP32, kind="ExternalInput").ap() for k, a in arrays.items()]
    out = nc.dram_tensor("out", (T, D), FP32, kind="ExternalOutput").ap()
    program(nc, *args, out)
    res = run_bass_kernel_spmd(nc, [{"in_" + k: a for k, a in arrays.items()}], core_ids=[0])
    return res.results[0]["out"].reshape(B, S, D)
```
